# Optimizing a Trainium2 kernel written in Bass

```python
import numpy as np
import jax
import jax.numpy as jnp

def _softmax(x, axis=-1):
    return jax.nn.softmax(x, axis=axis)

def _gelu(x):
    return jax.nn.gelu(x, approximate=True)

def _silu(x):
    return jax.nn.silu(x)

def _sigmoid(x):
    return jax.nn.sigmoid(x)

def _layernorm(x, axis=-1, eps=1e-05):
    m = jnp.mean(x, axis=axis, keepdims=True)
    v = jnp.var(x, axis=axis, keepdims=True)
    return (x - m) / jnp.sqrt(v + eps)

def _scatter_add(tgt, idx, src, axis=0):
    return tgt.at[idx].add(src)

def _segment_sum(src, seg, n):
    return jax.ops.segment_sum(src, seg, n)
kernel_name = 'mk_seq_preln_d4_jaxref_r8_4867f0'

def setup_inputs(seed: int=0):
    np.random.seed(seed)
    _w = jnp.asarray

    def _L0_attn_setup():
        import jax, jax.numpy as jnp
        import numpy as np
        NUM_BLOCKS = 4
        B, S, D = (4, 512, 128)
        A, FF = (128, 512)
        LN_EPS = 1e-06

        def _ln(x, s, b):
            m = jnp.mean(x, axis=-1, keepdims=True)
            v = jnp.mean(jnp.square(x - m), axis=-1, keepdims=True)
            return (x - m) * jax.lax.rsqrt(v + LN_EPS) * s + b
        key = jax.random.key(seed)
        ks = jax.random.split(key, 8)
        w = lambda k, shape: jax.random.normal(k, shape, dtype=jnp.float32) * 0.02
        return {'x': jax.random.normal(ks[0], (B, S, D), dtype=jnp.float32), 'Wq': w(ks[1], (NUM_BLOCKS, D, A)), 'bq': jnp.zeros((NUM_BLOCKS, A), jnp.float32), 'Wk': w(ks[2], (NUM_BLOCKS, D, A)), 'bk': jnp.zeros((NUM_BLOCKS, A), jnp.float32), 'Wv': w(ks[3], (NUM_BLOCKS, D, A)), 'bv': jnp.zeros((NUM_BLOCKS, A), jnp.float32), 'Wo': w(ks[4], (NUM_BLOCKS, A, D)), 'bo': jnp.zeros((NUM_BLOCKS, D), jnp.float32), 'ln1_s': jnp.ones((NUM_BLOCKS, D), jnp.float32), 'ln1_b': jnp.zeros((NUM_BLOCKS, D), jnp.float32), 'W1': w(ks[5], (NUM_BLOCKS, D, FF)), 'b1': jnp.zeros((NUM_BLOCKS, FF), jnp.float32), 'W2': w(ks[6], (NUM_BLOCKS, FF, D)), 'b2': jnp.zeros((NUM_BLOCKS, D), jnp.float32), 'ln2_s': jnp.ones((NUM_BLOCKS, D), jnp.float32), 'ln2_b': jnp.zeros((NUM_BLOCKS, D), jnp.float32)}
    _L0_attn_in = _L0_attn_setup()

    def _L0_ffn_setup():
        import jax, jax.numpy as jnp
        import numpy as np
        K = 2
        SCALING = 16.0 / 8.0
        key = jax.random.key(seed)
        ks = jax.random.split(key, 7)
        B, T, D, O, E, R = (4, 512, 128, 128, 8, 8)
        return {'x': jax.random.normal(ks[0], (B, T, D), dtype=jnp.float32), 'weight': jax.random.normal(ks[1], (O, D), dtype=jnp.float32) * (1.0 / np.sqrt(D)), 'bias': jax.random.normal(ks[2], (O,), dtype=jnp.float32) * 0.02, 'lora_A': jax.random.normal(ks[3], (E, R, D), dtype=jnp.float32) * (1.0 / np.sqrt(D)), 'lora_B': jax.random.normal(ks[4], (E, O, R), dtype=jnp.float32) * (1.0 / np.sqrt(R)), 'gate_w': jax.random.normal(ks[5], (E, D), dtype=jnp.float32) * 0.02, 'gate_b': jax.random.normal(ks[6], (E,), dtype=jnp.float32) * 0.02}
    _L0_ffn_in = _L0_ffn_setup()

    def _L1_attn_setup():
        import jax, jax.numpy as jnp
        import numpy as np
        B, T, D = (2, 256, 128)
        H = 16
        HD = D // H
        DL = 64
        NR = 64
        EPS = 1.1920929e-07

        def _rms_norm(x, w):
            ms = jnp.mean(jnp.square(x), axis=-1, keepdims=True)
            return x * jax.lax.rsqrt(ms + EPS) * w
        key = jax.random.key(seed)
        ks = jax.random.split(key, 10)
        s = 0.02
        return {'x': jax.random.normal(ks[0], (B, T, D), dtype=jnp.float32), 'W_DQ': jax.random.normal(ks[1], (DL, HD), dtype=jnp.float32) * s, 'W_UQ': jax.random.normal(ks[2], (HD, DL), dtype=jnp.float32) * s, 'W_DKV': jax.random.normal(ks[3], (2 * DL, HD), dtype=jnp.float32) * s, 'W_UKV': jax.random.normal(ks[4], (2 * HD, 2 * DL), dtype=jnp.float32) * s, 'W_QR': jax.random.normal(ks[5], (NR, HD), dtype=jnp.float32) * s, 'W_KR': jax.random.normal(ks[6], (NR, HD), dtype=jnp.float32) * s, 'W_O': jax.random.normal(ks[7], (HD, HD), dtype=jnp.float32) * s, 'q_norm_w': jnp.ones((HD,), dtype=jnp.float32), 'k_norm_w': jnp.ones((HD,), dtype=jnp.float32)}
    _L1_attn_in = _L1_attn_setup()

    def _L1_ffn_setup():
        import jax, jax.numpy as jnp
        import numpy as np
        B, SEQ, D, E, F = (4, 128, 128, 8, 512)
        CAPACITY = 2
        key = jax.random.key(seed)
        ks = jax.random.split(key, 8)
        x = jax.random.normal(ks[0], (B, SEQ, D), jnp.float32)
        gate_weight = jax.random.normal(ks[1], (E, D), jnp.float32) * 0.006
        W1 = jax.random.normal(ks[2], (E, D, F), jnp.float32) * (1.0 / np.sqrt(D))
        b1 = jnp.zeros((E, F), jnp.float32)
        W2 = jax.random.normal(ks[3], (E, F, D), jnp.float32) * (1.0 / np.sqrt(F))
        b2 = jnp.zeros((E, D), jnp.float32)
        Ws1 = jax.random.normal(ks[4], (D, F), jnp.float32) * (1.0 / np.sqrt(D))
        bs1 = jnp.zeros((F,), jnp.float32)
        Ws2 = jax.random.normal(ks[5], (F, D), jnp.float32) * (1.0 / np.sqrt(F))
        bs2 = jnp.zeros((D,), jnp.float32)
        return {'x': x, 'gate_weight': gate_weight, 'W1': W1, 'b1': b1, 'W2': W2, 'b2': b2, 'Ws1': Ws1, 'bs1': bs1, 'Ws2': Ws2, 'bs2': bs2}
    _L1_ffn_in = _L1_ffn_setup()

    def _L2_attn_setup():
        import jax, jax.numpy as jnp
        import numpy as np
        EPS = 1e-06
        H = 16

        def rmsnorm(x, w):
            return x * jax.lax.rsqrt(jnp.mean(x * x, axis=-1, keepdims=True) + EPS) * w

        def l2norm(x):
            return x * jax.lax.rsqrt(jnp.sum(x * x, axis=-1, keepdims=True) + EPS)

        def delta_rule(q, k, v, beta):
            B, S, Hh, dk = q.shape
            dv = v.shape[-1]
            qt = jnp.moveaxis(q, 1, 0)
            kt = jnp.moveaxis(k, 1, 0)
            vt = jnp.moveaxis(v, 1, 0)
            bt = jnp.moveaxis(beta, 1, 0)

            def step(Sm, inp):
                qi, ki, vi, bi = inp
                Sk = jnp.einsum('bhkv,bhk->bhv', Sm, ki)
                upd = ki[..., :, None] * (vi - Sk)[..., None, :]
                Sm = Sm + bi[..., None, None] * upd
                oi = jnp.einsum('bhkv,bhk->bhv', Sm, qi)
                return (Sm, oi)
            S0 = jnp.zeros((B, Hh, dk, dv), q.dtype)
            _, out = jax.lax.scan(step, S0, (qt, kt, vt, bt))
            return jnp.moveaxis(out, 0, 1)
        key = jax.random.key(seed)
        ks = jax.random.split(key, 12)
        B, S, D, F = (2, 256, 128, 512)
        std = 0.02
        inp = {'hidden_states': jax.random.normal(ks[0], (B, S, D), jnp.float32), 'Wq': jax.random.normal(ks[1], (D, D), jnp.float32) * std, 'Wk': jax.random.normal(ks[2], (D, D), jnp.float32) * std, 'Wv': jax.random.normal(ks[3], (D, D), jnp.float32) * std, 'Wb': jax.random.normal(ks[4], (D, H), jnp.float32) * std, 'Wo': jax.random.normal(ks[5], (D, D), jnp.float32) * std, 'ln1': jnp.ones((D,), jnp.float32), 'ln2': jnp.ones((D,), jnp.float32), 'Wg': jax.random.normal(ks[6], (D, F), jnp.float32) * std, 'Wu': jax.random.normal(ks[7], (D, F), jnp.float32) * std, 'Wd': jax.random.normal(ks[8], (F, D), jnp.float32) * std}
        return inp
    _L2_attn_in = _L2_attn_setup()

    def _L2_ffn_setup():
        import jax, jax.numpy as jnp
        import numpy as np
        DIM = 128

        def _reference_tuple_inner(x, W_r, W_k, W_v, mu_r, mu_k):
            B, T, C = x.shape
            x_prev = jnp.concatenate([jnp.zeros((B, 1, C), x.dtype), x[:, :-1, :]], axis=1)
            xr = mu_r * x + (1.0 - mu_r) * x_prev
            xk = mu_k * x + (1.0 - mu_k) * x_prev
            r = jax.nn.sigmoid(jnp.einsum('btc,dc->btd', xr, W_r))
            k = jnp.einsum('btc,dc->btd', xk, W_k)
            k_act = jnp.square(jax.nn.relu(k))
            out = r * jnp.einsum('btc,dc->btd', k_act, W_v)
            new_state = x[:, -1, :]
            return (out, new_state)
        key = jax.random.key(seed)
        ks = jax.random.split(key, 6)
        B, T, C = (8, 256, DIM)
        x = jax.random.normal(ks[0], (B, T, C), dtype=jnp.float32)
        s = 1.0 / np.sqrt(C)
        W_r = jax.random.uniform(ks[1], (C, C), jnp.float32, -s, s)
        W_k = jax.random.uniform(ks[2], (C, C), jnp.float32, -s, s)
        W_v = jax.random.uniform(ks[3], (C, C), jnp.float32, -s, s)
        mu_r = jax.random.uniform(ks[4], (C,), jnp.float32)
        mu_k = jax.random.uniform(ks[5], (C,), jnp.float32)
        return {'x': x, 'W_r': W_r, 'W_k': W_k, 'W_v': W_v, 'mu_r': mu_r, 'mu_k': mu_k}
    _L2_ffn_in = _L2_ffn_setup()

    def _L3_attn_setup():
        import jax, jax.numpy as jnp
        import numpy as np
        import math
        D_MODEL, N_HEADS, D_K, D_C, D_HR = (128, 8, 128, 32, 32)
        B, S = (4, 256)
        key = jax.random.key(seed)
        ks = jax.random.split(key, 17)

        def lin(k, fan_in, fan_out):
            lim = 1.0 / math.sqrt(fan_in)
            kw, kb = jax.random.split(k)
            W = jax.random.uniform(kw, (fan_in, fan_out), jnp.float32, -lim, lim)
            b = jax.random.uniform(kb, (fan_out,), jnp.float32, -lim, lim)
            return (W, b)
        W_DQ, b_DQ = lin(ks[0], D_MODEL, D_C)
        W_UQ, b_UQ = lin(ks[1], D_C, N_HEADS * D_K)
        W_DKV, b_DKV = lin(ks[2], D_MODEL, D_C)
        W_UK, b_UK = lin(ks[3], D_C, N_HEADS * D_K)
        W_UV, b_UV = lin(ks[4], D_C, N_HEADS * D_K)
        W_QR, b_QR = lin(ks[5], D_C, N_HEADS * D_HR)
        W_KR, b_KR = lin(ks[6], D_MODEL, D_HR)
        W_O, b_O = lin(ks[7], N_HEADS * D_K, D_MODEL)
        h_t = jax.random.normal(ks[8], (B, S, D_MODEL), jnp.float32)
        return {'h_t': h_t, 'W_DQ': W_DQ, 'b_DQ': b_DQ, 'W_UQ': W_UQ, 'b_UQ': b_UQ, 'W_DKV': W_DKV, 'b_DKV': b_DKV, 'W_UK': W_UK, 'b_UK': b_UK, 'W_UV': W_UV, 'b_UV': b_UV, 'W_QR': W_QR, 'b_QR': b_QR, 'W_KR': W_KR, 'b_KR': b_KR, 'W_O': W_O, 'b_O': b_O}
    _L3_attn_in = _L3_attn_setup()

    def _L3_ffn_setup():
        import jax, jax.numpy as jnp
        import numpy as np
        DIM = 128
        INTER = 64
        E = 16
        TOPK = 4
        N_GROUPS = 4
        TOPK_GROUPS = 2
        ROUTE_SCALE = 1.0
        INIT_STD = 0.02
        B, S = (2, 128)
        key = jax.random.key(seed)
        ks = jax.random.split(key, 8)
        return {'x': jax.random.normal(ks[0], (B, S, DIM), jnp.float32), 'gate_w': jax.random.normal(ks[1], (E, DIM), jnp.float32) * INIT_STD, 'gate_bias': jnp.zeros((E,), jnp.float32), 'w1': jax.random.normal(ks[2], (E, INTER, DIM), jnp.float32) * INIT_STD, 'w2': jax.random.normal(ks[3], (E, DIM, INTER), jnp.float32) * INIT_STD, 'w3': jax.random.normal(ks[4], (E, INTER, DIM), jnp.float32) * INIT_STD, 'ws1': jax.random.normal(ks[5], (INTER, DIM), jnp.float32) * INIT_STD, 'ws2': jax.random.normal(ks[6], (DIM, INTER), jnp.float32) * INIT_STD, 'ws3': jax.random.normal(ks[7], (INTER, DIM), jnp.float32) * INIT_STD}
    _L3_ffn_in = _L3_ffn_setup()
    _d = {'L0_attn_x': _L0_attn_in['x'], 'L0_attn_Wq': _L0_attn_in['Wq'], 'L0_attn_bq': _L0_attn_in['bq'], 'L0_attn_Wk': _L0_attn_in['Wk'], 'L0_attn_bk': _L0_attn_in['bk'], 'L0_attn_Wv': _L0_attn_in['Wv'], 'L0_attn_bv': _L0_attn_in['bv'], 'L0_attn_Wo': _L0_attn_in['Wo'], 'L0_attn_bo': _L0_attn_in['bo'], 'L0_attn_ln1_s': _L0_attn_in['ln1_s'], 'L0_attn_ln1_b': _L0_attn_in['ln1_b'], 'L0_attn_W1': _L0_attn_in['W1'], 'L0_attn_b1': _L0_attn_in['b1'], 'L0_attn_W2': _L0_attn_in['W2'], 'L0_attn_b2': _L0_attn_in['b2'], 'L0_attn_ln2_s': _L0_attn_in['ln2_s'], 'L0_attn_ln2_b': _L0_attn_in['ln2_b'], 'L0_ffn_weight': _L0_ffn_in['weight'], 'L0_ffn_bias': _L0_ffn_in['bias'], 'L0_ffn_lora_A': _L0_ffn_in['lora_A'], 'L0_ffn_lora_B': _L0_ffn_in['lora_B'], 'L0_ffn_gate_w': _L0_ffn_in['gate_w'], 'L0_ffn_gate_b': _L0_ffn_in['gate_b'], 'L1_attn_W_DQ': _L1_attn_in['W_DQ'], 'L1_attn_W_UQ': _L1_attn_in['W_UQ'], 'L1_attn_W_DKV': _L1_attn_in['W_DKV'], 'L1_attn_W_UKV': _L1_attn_in['W_UKV'], 'L1_attn_W_QR': _L1_attn_in['W_QR'], 'L1_attn_W_KR': _L1_attn_in['W_KR'], 'L1_attn_W_O': _L1_attn_in['W_O'], 'L1_attn_q_norm_w': _L1_attn_in['q_norm_w'], 'L1_attn_k_norm_w': _L1_attn_in['k_norm_w'], 'L1_ffn_gate_weight': _L1_ffn_in['gate_weight'], 'L1_ffn_W1': _L1_ffn_in['W1'], 'L1_ffn_b1': _L1_ffn_in['b1'], 'L1_ffn_W2': _L1_ffn_in['W2'], 'L1_ffn_b2': _L1_ffn_in['b2'], 'L1_ffn_Ws1': _L1_ffn_in['Ws1'], 'L1_ffn_bs1': _L1_ffn_in['bs1'], 'L1_ffn_Ws2': _L1_ffn_in['Ws2'], 'L1_ffn_bs2': _L1_ffn_in['bs2'], 'L2_attn_Wq': _L2_attn_in['Wq'], 'L2_attn_Wk': _L2_attn_in['Wk'], 'L2_attn_Wv': _L2_attn_in['Wv'], 'L2_attn_Wb': _L2_attn_in['Wb'], 'L2_attn_Wo': _L2_attn_in['Wo'], 'L2_attn_ln1': _L2_attn_in['ln1'], 'L2_attn_ln2': _L2_attn_in['ln2'], 'L2_attn_Wg': _L2_attn_in['Wg'], 'L2_attn_Wu': _L2_attn_in['Wu'], 'L2_attn_Wd': _L2_attn_in['Wd'], 'L2_ffn_W_r': _L2_ffn_in['W_r'], 'L2_ffn_W_k': _L2_ffn_in['W_k'], 'L2_ffn_W_v': _L2_ffn_in['W_v'], 'L2_ffn_mu_r': _L2_ffn_in['mu_r'], 'L2_ffn_mu_k': _L2_ffn_in['mu_k'], 'L3_attn_W_DQ': _L3_attn_in['W_DQ'], 'L3_attn_b_DQ': _L3_attn_in['b_DQ'], 'L3_attn_W_UQ': _L3_attn_in['W_UQ'], 'L3_attn_b_UQ': _L3_attn_in['b_UQ'], 'L3_attn_W_DKV': _L3_attn_in['W_DKV'], 'L3_attn_b_DKV': _L3_attn_in['b_DKV'], 'L3_attn_W_UK': _L3_attn_in['W_UK'], 'L3_attn_b_UK': _L3_attn_in['b_UK'], 'L3_attn_W_UV': _L3_attn_in['W_UV'], 'L3_attn_b_UV': _L3_attn_in['b_UV'], 'L3_attn_W_QR': _L3_attn_in['W_QR'], 'L3_attn_b_QR': _L3_attn_in['b_QR'], 'L3_attn_W_KR': _L3_attn_in['W_KR'], 'L3_attn_b_KR': _L3_attn_in['b_KR'], 'L3_attn_W_O': _L3_attn_in['W_O'], 'L3_attn_b_O': _L3_attn_in['b_O'], 'L3_ffn_gate_w': _L3_ffn_in['gate_w'], 'L3_ffn_gate_bias': _L3_ffn_in['gate_bias'], 'L3_ffn_w1': _L3_ffn_in['w1'], 'L3_ffn_w2': _L3_ffn_in['w2'], 'L3_ffn_w3': _L3_ffn_in['w3'], 'L3_ffn_ws1': _L3_ffn_in['ws1'], 'L3_ffn_ws2': _L3_ffn_in['ws2'], 'L3_ffn_ws3': _L3_ffn_in['ws3']}
    _x0 = _d['L0_attn_x']
    _d['L0_attn_x'] = jax.random.normal(jax.random.fold_in(jax.random.key(seed), 1), (32, 256, 128), dtype=_x0.dtype)
    del _x0
    return _d

def reference(L0_attn_x, L0_attn_Wq, L0_attn_bq, L0_attn_Wk, L0_attn_bk, L0_attn_Wv, L0_attn_bv, L0_attn_Wo, L0_attn_bo, L0_attn_ln1_s, L0_attn_ln1_b, L0_attn_W1, L0_attn_b1, L0_attn_W2, L0_attn_b2, L0_attn_ln2_s, L0_attn_ln2_b, L0_ffn_weight, L0_ffn_bias, L0_ffn_lora_A, L0_ffn_lora_B, L0_ffn_gate_w, L0_ffn_gate_b, L1_attn_W_DQ, L1_attn_W_UQ, L1_attn_W_DKV, L1_attn_W_UKV, L1_attn_W_QR, L1_attn_W_KR, L1_attn_W_O, L1_attn_q_norm_w, L1_attn_k_norm_w, L1_ffn_gate_weight, L1_ffn_W1, L1_ffn_b1, L1_ffn_W2, L1_ffn_b2, L1_ffn_Ws1, L1_ffn_bs1, L1_ffn_Ws2, L1_ffn_bs2, L2_attn_Wq, L2_attn_Wk, L2_attn_Wv, L2_attn_Wb, L2_attn_Wo, L2_attn_ln1, L2_attn_ln2, L2_attn_Wg, L2_attn_Wu, L2_attn_Wd, L2_ffn_W_r, L2_ffn_W_k, L2_ffn_W_v, L2_ffn_mu_r, L2_ffn_mu_k, L3_attn_W_DQ, L3_attn_b_DQ, L3_attn_W_UQ, L3_attn_b_UQ, L3_attn_W_DKV, L3_attn_b_DKV, L3_attn_W_UK, L3_attn_b_UK, L3_attn_W_UV, L3_attn_b_UV, L3_attn_W_QR, L3_attn_b_QR, L3_attn_W_KR, L3_attn_b_KR, L3_attn_W_O, L3_attn_b_O, L3_ffn_gate_w, L3_ffn_gate_bias, L3_ffn_w1, L3_ffn_w2, L3_ffn_w3, L3_ffn_ws1, L3_ffn_ws2, L3_ffn_ws3):

    def _L0_attn_ref(x, Wq, bq, Wk, bk, Wv, bv, Wo, bo, ln1_s, ln1_b, W1, b1, W2, b2, ln2_s, ln2_b):
        import jax, jax.numpy as jnp
        import numpy as np
        NUM_BLOCKS = 4
        B, S, D = (4, 512, 128)
        A, FF = (128, 512)
        LN_EPS = 1e-06

        def _ln(x, s, b):
            m = jnp.mean(x, axis=-1, keepdims=True)
            v = jnp.mean(jnp.square(x - m), axis=-1, keepdims=True)
            return (x - m) * jax.lax.rsqrt(v + LN_EPS) * s + b
        for i in range(NUM_BLOCKS):
            residual = x
            q = x @ Wq[i] + bq[i]
            k = x @ Wk[i] + bk[i]
            v = x @ Wv[i] + bv[i]
            Q = jax.nn.elu(q) + 1.0
            K = jax.nn.elu(k) + 1.0
            KV = jnp.einsum('nsh,nsh->nh', K, v, precision='highest')
            Ksum = jnp.sum(K, axis=1)
            Z = 1.0 / (Q * Ksum[:, None, :] + 1e-06)
            V = Q * KV[:, None, :] * Z
            a = jax.nn.gelu(V @ Wo[i] + bo[i])
            a = jax.nn.gelu(a)
            x = _ln(a + residual, ln1_s[i], ln1_b[i])
            residual = x
            h = jax.nn.gelu(x @ W1[i] + b1[i])
            f = jax.nn.gelu(h @ W2[i] + b2[i])
            x = _ln(f + residual, ln2_s[i], ln2_b[i])
        return x

    def _L0_ffn_ref(x, weight, bias, lora_A, lora_B, gate_w, gate_b):
        import jax, jax.numpy as jnp
        import numpy as np
        K = 2
        SCALING = 16.0 / 8.0
        orig_shape = x.shape
        D = orig_shape[-1]
        x_flat = x.reshape(-1, D)
        base_out = x_flat @ weight.T + bias
        logits = x_flat @ gate_w.T + gate_b
        topk_logits, topk_idx = jax.lax.top_k(logits, K)
        topk_gates = jax.nn.softmax(topk_logits, axis=-1)
        xA = jnp.einsum('nd,erd->ner', x_flat, lora_A)
        delta_all = jnp.einsum('ner,eor->neo', xA, lora_B)
        delta_topk = jnp.take_along_axis(delta_all, topk_idx[:, :, None], axis=1)
        lora_update = jnp.sum(delta_topk * topk_gates[:, :, None], axis=1)
        out_flat = base_out + SCALING * lora_update
        return out_flat.reshape(*orig_shape[:-1], weight.shape[0])

    def _L1_attn_ref(x, W_DQ, W_UQ, W_DKV, W_UKV, W_QR, W_KR, W_O, q_norm_w, k_norm_w):
        import jax, jax.numpy as jnp
        import numpy as np
        B, T, D = (2, 256, 128)
        H = 16
        HD = D // H
        DL = 64
        NR = 64
        EPS = 1.1920929e-07

        def _rms_norm(x, w):
            ms = jnp.mean(jnp.square(x), axis=-1, keepdims=True)
            return x * jax.lax.rsqrt(ms + EPS) * w
        b, t, d = x.shape
        scale = HD ** (-0.5)
        xh = x.reshape(b, t, H, HD).transpose(0, 2, 1, 3)
        c_q = jnp.einsum('bhtd,ld->bhtl', xh, W_DQ)
        q_c = jnp.einsum('bhtl,dl->bhtd', c_q, W_UQ)
        q_c_norm = _rms_norm(q_c, q_norm_w)
        q_r = jnp.einsum('bhtd,rd->bhtr', q_c_norm, W_QR)
        q = jnp.concatenate([q_c_norm, q_r], axis=-1)
        c_kv = jnp.einsum('bhtd,ld->bhtl', xh, W_DKV)
        kv = jnp.einsum('bhtl,dl->bhtd', c_kv, W_UKV)
        k_c, v_c = (kv[..., :HD], kv[..., HD:])
        k_c_norm = _rms_norm(k_c, k_norm_w)
        k_r = jnp.einsum('bhtd,rd->bhtr', xh, W_KR)
        k = jnp.concatenate([k_c_norm, k_r], axis=-1)
        scores = jnp.einsum('bhqd,bhkd->bhqk', q, k) * scale
        causal = jnp.triu(jnp.full((t, t), -jnp.inf, dtype=scores.dtype), k=1)
        attn = jax.nn.softmax(scores + causal, axis=-1)
        ctx = jnp.einsum('bhqk,bhkd->bhqd', attn, v_c)
        out = jnp.einsum('bhtd,od->bhto', ctx, W_O)
        return out.transpose(0, 2, 1, 3).reshape(b, t, d)

    def _L1_ffn_ref(x, gate_weight, W1, b1, W2, b2, Ws1, bs1, Ws2, bs2):
        import jax, jax.numpy as jnp
        import numpy as np
        B, SEQ, D, E, F = (4, 128, 128, 8, 512)
        CAPACITY = 2
        Bb, s, Dd = x.shape
        Ee = gate_weight.shape[0]
        xf = x.reshape(-1, Dd)
        S = xf.shape[0]
        logits = xf @ gate_weight.T
        scores = jax.nn.softmax(logits, axis=-1).T
        k = S * CAPACITY
        vals, idx = jax.lax.top_k(scores.reshape(-1), k)
        eidx = idx // S
        tidx = idx % S
        gate = jnp.zeros((Ee, S), x.dtype).at[eidx, tidx].add(vals)
        h = jax.nn.gelu(jnp.einsum('sd,edf->esf', xf, W1) + b1[:, None, :], approximate=True)
        y = jnp.einsum('esf,efd->esd', h, W2) + b2[:, None, :]
        out = jnp.einsum('es,esd->sd', gate, y)
        shared = jax.nn.gelu(xf @ Ws1 + bs1, approximate=True) @ Ws2 + bs2
        out = out + shared
        return out.reshape(Bb, s, Dd)

    def _L2_attn_ref(hidden_states, Wq, Wk, Wv, Wb, Wo, ln1, ln2, Wg, Wu, Wd):
        import jax, jax.numpy as jnp
        import numpy as np
        EPS = 1e-06
        H = 16

        def rmsnorm(x, w):
            return x * jax.lax.rsqrt(jnp.mean(x * x, axis=-1, keepdims=True) + EPS) * w

        def l2norm(x):
            return x * jax.lax.rsqrt(jnp.sum(x * x, axis=-1, keepdims=True) + EPS)

        def delta_rule(q, k, v, beta):
            B, S, Hh, dk = q.shape
            dv = v.shape[-1]
            qt = jnp.moveaxis(q, 1, 0)
            kt = jnp.moveaxis(k, 1, 0)
            vt = jnp.moveaxis(v, 1, 0)
            bt = jnp.moveaxis(beta, 1, 0)

            def step(Sm, inp):
                qi, ki, vi, bi = inp
                Sk = jnp.einsum('bhkv,bhk->bhv', Sm, ki)
                upd = ki[..., :, None] * (vi - Sk)[..., None, :]
                Sm = Sm + bi[..., None, None] * upd
                oi = jnp.einsum('bhkv,bhk->bhv', Sm, qi)
                return (Sm, oi)
            S0 = jnp.zeros((B, Hh, dk, dv), q.dtype)
            _, out = jax.lax.scan(step, S0, (qt, kt, vt, bt))
            return jnp.moveaxis(out, 0, 1)
        B, S, D = hidden_states.shape
        dk = D // H
        x = rmsnorm(hidden_states, ln1)
        q = l2norm(jax.nn.silu(x @ Wq).reshape(B, S, H, dk))
        k = l2norm(jax.nn.silu(x @ Wk).reshape(B, S, H, dk))
        v = jax.nn.silu(x @ Wv).reshape(B, S, H, dk)
        beta = jax.nn.sigmoid(x @ Wb)
        o = delta_rule(q, k, v, beta).reshape(B, S, D)
        h = hidden_states + o @ Wo
        y = rmsnorm(h, ln2)
        h = h + jax.nn.silu(y @ Wg) * (y @ Wu) @ Wd
        return h

    def _L2_ffn_ref(x, W_r, W_k, W_v, mu_r, mu_k):
        import jax, jax.numpy as jnp
        import numpy as np
        DIM = 128

        def _reference_tuple_inner(x, W_r, W_k, W_v, mu_r, mu_k):
            B, T, C = x.shape
            x_prev = jnp.concatenate([jnp.zeros((B, 1, C), x.dtype), x[:, :-1, :]], axis=1)
            xr = mu_r * x + (1.0 - mu_r) * x_prev
            xk = mu_k * x + (1.0 - mu_k) * x_prev
            r = jax.nn.sigmoid(jnp.einsum('btc,dc->btd', xr, W_r))
            k = jnp.einsum('btc,dc->btd', xk, W_k)
            k_act = jnp.square(jax.nn.relu(k))
            out = r * jnp.einsum('btc,dc->btd', k_act, W_v)
            new_state = x[:, -1, :]
            return (out, new_state)
        return _reference_tuple_inner(x, W_r, W_k, W_v, mu_r, mu_k)[0]

    def _L3_attn_ref(h_t, W_DQ, b_DQ, W_UQ, b_UQ, W_DKV, b_DKV, W_UK, b_UK, W_UV, b_UV, W_QR, b_QR, W_KR, b_KR, W_O, b_O):
        import jax, jax.numpy as jnp
        import numpy as np
        import math
        D_MODEL, N_HEADS, D_K, D_C, D_HR = (128, 8, 128, 32, 32)
        B, S = (4, 256)
        b, s, _ = h_t.shape
        c_q = h_t @ W_DQ + b_DQ
        c_kv = h_t @ W_DKV + b_DKV
        q_c = (c_q @ W_UQ + b_UQ).reshape(b, s, N_HEADS, D_K).transpose(0, 2, 1, 3)
        k_c = (c_kv @ W_UK + b_UK).reshape(b, s, N_HEADS, D_K).transpose(0, 2, 1, 3)
        v_c = (c_kv @ W_UV + b_UV).reshape(b, s, N_HEADS, D_K).transpose(0, 2, 1, 3)
        q_r = (c_q @ W_QR + b_QR).reshape(b, s, N_HEADS, D_HR).transpose(0, 2, 1, 3)
        k_r = (h_t @ W_KR + b_KR)[:, None, :, :]
        k_r = jnp.broadcast_to(k_r, (b, N_HEADS, s, D_HR))
        q = jnp.concatenate([q_c, q_r], axis=-1)
        k = jnp.concatenate([k_c, k_r], axis=-1)
        scale = 1.0 / math.sqrt(D_K + D_HR)
        scores = jnp.einsum('bhsd,bhtd->bhst', q, k) * scale
        attn = jax.nn.softmax(scores, axis=-1)
        o = jnp.einsum('bhst,bhtd->bhsd', attn, v_c)
        o = o.transpose(0, 2, 1, 3).reshape(b, s, N_HEADS * D_K)
        return o @ W_O + b_O

    def _L3_ffn_ref(x, gate_w, gate_bias, w1, w2, w3, ws1, ws2, ws3):
        import jax, jax.numpy as jnp
        import numpy as np
        DIM = 128
        INTER = 64
        E = 16
        TOPK = 4
        N_GROUPS = 4
        TOPK_GROUPS = 2
        ROUTE_SCALE = 1.0
        INIT_STD = 0.02
        B, S = (2, 128)
        Bx, Sx, D = x.shape
        T = Bx * Sx
        xf = x.reshape(T, D)
        scores = jax.nn.sigmoid(xf @ gate_w.T)
        original_scores = scores
        s = scores + gate_bias
        sg = s.reshape(T, N_GROUPS, E // N_GROUPS)
        group_scores = sg.max(axis=-1)
        _, gidx = jax.lax.top_k(group_scores, TOPK_GROUPS)
        keep = jnp.zeros((T, N_GROUPS), bool).at[jnp.arange(T)[:, None], gidx].set(True)
        s_masked = jnp.where(keep[:, :, None], sg, -jnp.inf).reshape(T, E)
        _, idx = jax.lax.top_k(s_masked, TOPK)
        weights = jnp.take_along_axis(original_scores, idx, axis=1) * ROUTE_SCALE
        comb = jnp.zeros((T, E), x.dtype).at[jnp.arange(T)[:, None], idx].add(weights)
        h1 = jnp.einsum('td,eid->tei', xf, w1)
        h3 = jnp.einsum('td,eid->tei', xf, w3)
        h = jax.nn.silu(h1) * h3
        y = jnp.einsum('tei,edi,te->td', h, w2, comb)
        z = jax.nn.silu(xf @ ws1.T) * (xf @ ws3.T) @ ws2.T
        return (y + z).reshape(Bx, Sx, D)
    x = L0_attn_x
    x = x + _L0_attn_ref(_layernorm(x, axis=-1), L0_attn_Wq, L0_attn_bq, L0_attn_Wk, L0_attn_bk, L0_attn_Wv, L0_attn_bv, L0_attn_Wo, L0_attn_bo, L0_attn_ln1_s, L0_attn_ln1_b, L0_attn_W1, L0_attn_b1, L0_attn_W2, L0_attn_b2, L0_attn_ln2_s, L0_attn_ln2_b)
    x = x + _L0_ffn_ref(_layernorm(x, axis=-1), L0_ffn_weight, L0_ffn_bias, L0_ffn_lora_A, L0_ffn_lora_B, L0_ffn_gate_w, L0_ffn_gate_b)
    x = x + _L1_attn_ref(_layernorm(x, axis=-1), L1_attn_W_DQ, L1_attn_W_UQ, L1_attn_W_DKV, L1_attn_W_UKV, L1_attn_W_QR, L1_attn_W_KR, L1_attn_W_O, L1_attn_q_norm_w, L1_attn_k_norm_w)
    x = x + _L1_ffn_ref(_layernorm(x, axis=-1), L1_ffn_gate_weight, L1_ffn_W1, L1_ffn_b1, L1_ffn_W2, L1_ffn_b2, L1_ffn_Ws1, L1_ffn_bs1, L1_ffn_Ws2, L1_ffn_bs2)
    x = x + _L2_attn_ref(_layernorm(x, axis=-1), L2_attn_Wq, L2_attn_Wk, L2_attn_Wv, L2_attn_Wb, L2_attn_Wo, L2_attn_ln1, L2_attn_ln2, L2_attn_Wg, L2_attn_Wu, L2_attn_Wd)
    x = x + _L2_ffn_ref(_layernorm(x, axis=-1), L2_ffn_W_r, L2_ffn_W_k, L2_ffn_W_v, L2_ffn_mu_r, L2_ffn_mu_k)
    x = x + _L3_attn_ref(_layernorm(x, axis=-1), L3_attn_W_DQ, L3_attn_b_DQ, L3_attn_W_UQ, L3_attn_b_UQ, L3_attn_W_DKV, L3_attn_b_DKV, L3_attn_W_UK, L3_attn_b_UK, L3_attn_W_UV, L3_attn_b_UV, L3_attn_W_QR, L3_attn_b_QR, L3_attn_W_KR, L3_attn_b_KR, L3_attn_W_O, L3_attn_b_O)
    x = x + _L3_ffn_ref(_layernorm(x, axis=-1), L3_ffn_gate_w, L3_ffn_gate_bias, L3_ffn_w1, L3_ffn_w2, L3_ffn_w3, L3_ffn_ws1, L3_ffn_ws2, L3_ffn_ws3)
    return x

_drawn_inputs = setup_inputs


def setup_inputs(seed=0):
    import zlib

    import numpy as np

    out = dict(_drawn_inputs(seed))
    spreads = {'L0_attn_bq': (0.0, 2.0),
     'L0_attn_bk': (0.0, 0.8),
     'L0_attn_bv': (0.0, 0.1),
     'L0_attn_bo': (0.0, 0.1),
     'L0_attn_ln1_s': (1.0, 0.2),
     'L0_attn_ln1_b': (0.0, 0.1),
     'L0_attn_b1': (0.0, 0.1),
     'L0_attn_b2': (0.0, 0.1),
     'L0_attn_ln2_s': (1.0, 0.2),
     'L0_attn_ln2_b': (0.0, 0.1),
     'L1_attn_q_norm_w': (1.0, 0.6),
     'L1_attn_k_norm_w': (1.0, 0.6),
     'L1_ffn_b1': (0.0, 0.8),
     'L1_ffn_b2': (0.0, 0.8),
     'L1_ffn_bs1': (0.0, 0.345),
     'L1_ffn_bs2': (0.0, 0.1),
     'L2_attn_ln1': (1.0, 0.6),
     'L2_attn_ln2': (1.0, 0.6),
     'L3_ffn_gate_bias': (0.0, 0.8)}
    factors = {'L0_attn_Wq': 64.0,
     'L0_attn_Wk': 5.302,
     'L0_ffn_bias': 6.584,
     'L1_attn_W_DQ': 8.0,
     'L1_attn_W_UQ': 8.0,
     'L1_attn_W_DKV': 8.0,
     'L1_attn_W_UKV': 8.0,
     'L1_attn_W_QR': 8.0,
     'L1_attn_W_KR': 8.0,
     'L1_attn_W_O': 8.0,
     'L2_attn_Wq': 8.0,
     'L2_attn_Wk': 8.0,
     'L2_attn_Wv': 8.0,
     'L2_attn_Wb': 8.0,
     'L2_attn_Wo': 8.0,
     'L2_attn_Wg': 8.0,
     'L2_attn_Wu': 8.0,
     'L2_attn_Wd': 8.0,
     'L2_ffn_W_r': 8.0,
     'L2_ffn_W_k': 2.73,
     'L2_ffn_mu_r': 8.0,
     'L2_ffn_mu_k': 4.251,
     'L3_attn_W_DQ': 8.0,
     'L3_attn_b_DQ': 8.0,
     'L3_attn_W_UQ': 8.0,
     'L3_attn_b_UQ': 8.0,
     'L3_attn_W_DKV': 6.612,
     'L3_attn_b_DKV': 8.0,
     'L3_attn_W_UK': 8.0,
     'L3_attn_b_UK': 64.0,
     'L3_attn_W_UV': 6.571,
     'L3_attn_b_UV': 9.684,
     'L3_attn_W_QR': 8.0,
     'L3_attn_b_QR': 8.0,
     'L3_attn_W_KR': 8.0,
     'L3_attn_b_KR': 64.0,
     'L3_attn_W_O': 2.868,
     'L3_attn_b_O': 64.0,
     'L3_ffn_gate_w': 8.0,
     'L3_ffn_w1': 8.0,
     'L3_ffn_w2': 8.0,
     'L3_ffn_w3': 8.0,
     'L3_ffn_ws1': 8.0,
     'L3_ffn_ws2': 8.0,
     'L3_ffn_ws3': 8.0}
    for name, (base, spread) in spreads.items():
        noise = np.random.default_rng([zlib.crc32(name.encode()), seed]).standard_normal(out[name].shape)
        drawn = base * np.exp(spread * noise) if base else spread * noise
        out[name] = jnp.asarray(drawn.astype(out[name].dtype))
    for name, factor in factors.items():
        out[name] = (out[name] * factor).astype(out[name].dtype)
    return out
```

```python
from contextlib import ExitStack

import concourse.bass as bass
from concourse import mybir

FP32 = mybir.dt.float32
I32 = mybir.dt.int32
ACT = mybir.ActivationFunctionType
ALU = mybir.AluOpType
AX = mybir.AxisListType

P = 128
B, S = 32, 256
TOK = B * S
C = 512
SEQ = C // S
NCH = TOK // C
STREAMS = 2
TRIPS = NCH // STREAMS
TPC = C // P
NT = TOK // P


class Stage:

    def __init__(self, nc, name):
        self.nc, self.name, self.stack, self.sems = nc, name, ExitStack(), []

    def __enter__(self):
        return self

    def __exit__(self, *failure):
        self.stack.close()
        if failure[0] is None:
            self.nc.clear_and_free_semaphores(self.sems)
            self.nc.all_engine_barrier()

    def sbuf(self, name, shape, dtype=FP32):
        return self.stack.enter_context(self.nc.sbuf_tensor(f"{self.name}_{name}", shape, dtype))

    def psum(self, name, shape, dtype=FP32):
        return self.stack.enter_context(self.nc.psum_tensor(f"{self.name}_{name}", shape, dtype))

    def sem(self, name):
        self.sems.append(self.nc.alloc_semaphore(f"{self.name}_{name}"))
        return self.sems[-1]

    def sem_each(self, name):
        return [self.sem(f"{name}{s}") for s in range(STREAMS)]


class Chain:

    def __init__(self, eng, sem, trip, per_trip):
        self.eng, self.sem, self.base, self.n, self.per_trip = eng, sem, trip * per_trip, 0, per_trip

    def mark(self, instruction):
        instruction.then_inc(self.sem, 1)
        self.n += 1
        return self.n

    def wait(self, n=None):
        self.eng.wait_ge(self.sem, self.base + (self.n if n is None else n))

    def close(self):
        assert self.n == self.per_trip, (self.sem, self.n)


def chunk_of(x, trip, s):
    return x[:, bass.ds((trip * STREAMS + s) * C, C)]


def chunk_at(x, chunk):
    return x[:, bass.ds(chunk * C, C)]


def seqs(ap):
    return ap.rearrange("p (b t) -> p b t", b=SEQ)


def make_constants(nc, k):
    with Stage(nc, "const") as st:
        zeroed, ident_done = st.sem("zeroed"), st.sem("ident_done")
        with nc.Block() as block:

            @block.gpsimd
            def _(pool):
                nc.gpsimd.memset(k.mean[:, :], 1.0 / P)
                nc.gpsimd.memset(k.minus_half[:, :], -0.5)
                nc.gpsimd.memset(k.lower[:, :, :], 1.0).then_inc(zeroed, 1)
                nc.gpsimd.memset(k.ident[:, :], 0.0).then_inc(zeroed, 1)
                pool.wait_ge(zeroed, 2)
                nc.gpsimd.affine_select(out=k.ident[:, :], in_=k.ident[:, :], compare_op=ALU.not_equal,
                                        fill=1.0, base=0, pattern=[[-1, P]],
                                        channel_multiplier=1).then_inc(ident_done, 1)
                nc.gpsimd.affine_select(out=k.lower[:, :, :], in_=k.lower[:, :, :], compare_op=ALU.is_gt,
                                        fill=0.0, base=0, pattern=[[1, 16], [-1, 16]],
                                        channel_multiplier=0).then_inc(ident_done, 1)
                pool.wait_ge(ident_done, 2)


class NormSems:

    def __init__(self, st):
        self.mean_ready = st.sem("ln_mean_ready")
        self.centred_ready = st.sem("ln_centred_ready")
        self.square_ready = st.sem("ln_square_ready")
        self.var_ready = st.sem("ln_var_ready")
        self.vareps_ready = st.sem("ln_vareps_ready")
        self.rstd_ready = st.sem("ln_rstd_ready")
        self.spread_ready = st.sem("ln_spread_ready")
        self.normed_ready = st.sem("ln_normed_ready")



def norm_pe_mean(nc, k, ns, src, mean_ps):
    nc.tensor.matmul(mean_ps, k.mean[:, :], src, start=True, stop=True).then_inc(ns.mean_ready, 1)


def norm_pe_var(nc, pe, k, ns, at, square, var_ps):
    pe.wait_ge(ns.square_ready, at)
    for t in range(TPC):
        mm = nc.tensor.matmul(var_ps[:, t:t + 1], square[:, t * P:(t + 1) * P], k.mean[:, 0:1],
                              start=True, stop=True)
    mm.then_inc(ns.var_ready, 1)


def norm_pe_spread(nc, pe, k, ns, at, rstd, spread_ps):
    pe.wait_ge(ns.rstd_ready, at)
    for t in range(TPC):
        mm = nc.tensor.transpose(spread_ps[:, t * P:(t + 1) * P], rstd[:, t:t + 1].to_broadcast([P, P]),
                                 k.ident[:, :])
    mm.then_inc(ns.spread_ready, 1)


def norm_dve_centre(nc, dve, ns, at, src, mean_ps, centred):
    dve.wait_ge(ns.mean_ready, at)
    nc.vector.tensor_tensor(centred, src, mean_ps, ALU.subtract).then_inc(ns.centred_ready, 1)


def norm_act_square(nc, act, ns, at, centred, square):
    act.wait_ge(ns.centred_ready, at)
    nc.scalar.activation(square, centred, ACT.Square).then_inc(ns.square_ready, 1)


def norm_dve_vareps(nc, dve, ns, at, var_ps, vareps, eps):
    dve.wait_ge(ns.var_ready, at)
    nc.vector.tensor_scalar(vareps, var_ps[:, 0:TPC], eps, None, ALU.add).then_inc(ns.vareps_ready, 1)


def norm_pool_rstd(nc, pool, k, ns, at, vareps, rstd):
    pool.wait_ge(ns.vareps_ready, at)
    nc.gpsimd.tensor_tensor(rstd, vareps, k.minus_half[:, 0:TPC], ALU.pow).then_inc(ns.rstd_ready, 1)


def norm_dve_scale(nc, dve, ns, at, centred, gain, spread_ps, out):
    dve.wait_ge(ns.spread_ready, at)
    nc.vector.scalar_tensor_tensor(out, centred, gain, spread_ps,
                                   ALU.mult, ALU.mult).then_inc(ns.normed_ready, 1)


def l0_attention(nc, k, w_dram, x):
    NB, FF, HT = 4, 512, 4
    LN_PER_TRIP = 1 + 2 * NB
    with Stage(nc, "l0a") as st:
        ncol = w_dram.shape[1]
        w = st.sbuf("w", [P, ncol])
        o, cut = 0, {}
        for name, width in (("wq", P), ("wk", P), ("wv", P), ("wo", P), ("w1", FF), ("w2", FF),
                            ("bq", 1), ("bk", 1), ("bv", 1), ("bo", 1), ("s1", 1), ("c1", 1),
                            ("b1", HT), ("b2", 1), ("s2", 1), ("c2", 1)):
            cut[name] = (o, width)
            o += NB * width
        assert o == ncol

        def wt(name, i, a=0, n=None):
            o, width = cut[name]
            o += i * width + a
            return w[:, o:o + (width if n is None else n)]

        two = range(STREAMS)
        y = [st.sbuf(f"y{s}", [P, C]) for s in two]
        cen = [st.sbuf(f"cen{s}", [P, C]) for s in two]
        sq = [st.sbuf(f"sq{s}", [P, C]) for s in two]
        vareps = [st.sbuf(f"vareps{s}", [P, TPC]) for s in two]
        rstd = [st.sbuf(f"rstd{s}", [P, TPC]) for s in two]
        eq = [st.sbuf(f"eq{s}", [P, C]) for s in two]
        ek = [st.sbuf(f"ek{s}", [P, C]) for s in two]
        qq = [st.sbuf(f"qq{s}", [P, C]) for s in two]
        kk = [st.sbuf(f"kk{s}", [P, C]) for s in two]
        junk = [st.sbuf(f"junk{s}", [P, C]) for s in two]
        vv = [st.sbuf(f"vv{s}", [P, C]) for s in two]
        den = [st.sbuf(f"den{s}", [P, C]) for s in two]
        ga = [st.sbuf(f"ga{s}", [P, C]) for s in two]
        h = [st.sbuf(f"h{s}", [P, HT, C]) for s in two]
        ksum = [st.sbuf(f"ksum{s}", [P, SEQ]) for s in two]
        kv = [st.sbuf(f"kv{s}", [P, SEQ]) for s in two]
        bank = [[st.psum(f"ps{s}{j}", [P, C]) for j in range(4)] for s in two]

        loaded = st.sem("loaded")
        ns = NormSems(st)
        y_ready = st.sem("y_ready")
        qkv_ready = st.sem("qkv_ready")
        exp_ready = st.sem("exp_ready")
        v_ready = st.sem("v_ready")
        o_ready = st.sem("o_ready")
        gelu1 = st.sem("gelu1")
        a_ready = st.sem("a_ready")
        t_ready = st.sem("t_ready")
        h_ready = st.sem("h_ready")
        hg_ready = st.sem("hg_ready")
        f_ready = st.sem("f_ready")
        dve_step = st.sem("dve_step")
        done = st.sem("done")

        with nc.Block() as block:

            @block.sync
            def _(sp):
                sp.dma_start(w[:, :], w_dram).then_inc(loaded, 16)

            @block.tensor
            def _(pe):
                pe.wait_ge(loaded, 16)
                with pe.Fori(0, TRIPS) as trip:
                    ln = trip * (LN_PER_TRIP * STREAMS)

                    def norm(n, src, m, v):
                        for s in two:
                            if n:
                                pe.wait_ge(t_ready, trip * (2 * NB * STREAMS) + (n - 1) * STREAMS + s + 1)
                            norm_pe_mean(nc, k, ns, src(s), bank[s][m][:, :])
                        for s in two:
                            norm_pe_var(nc, pe, k, ns, ln + n * STREAMS + s + 1, sq[s][:, :], bank[s][v][:, :])
                        for s in two:
                            norm_pe_spread(nc, pe, k, ns, ln + n * STREAMS + s + 1, rstd[s][:, :], bank[s][m][:, :])

                    pe.wait_ge(done, trip * STREAMS + 1)
                    norm(0, lambda s: chunk_of(x, trip, s), 0, 1)
                    for i in range(NB):
                        for s in two:
                            pe.wait_ge(y_ready, ln + 2 * i * STREAMS + s + 1)
                            for j, name in enumerate(("wq", "wk", "wv")):
                                nc.tensor.matmul(bank[s][j][:, :], wt(name, i), y[s][:, :],
                                                 start=True, stop=True).then_inc(qkv_ready, 1)
                        for s in two:
                            pe.wait_ge(v_ready, (trip * NB + i) * STREAMS + s + 1)
                            nc.tensor.matmul(bank[s][3][:, :], wt("wo", i), vv[s][:, :],
                                             start=True, stop=True).then_inc(o_ready, 1)
                        norm(2 * i + 1, lambda s: ga[s][:, :], 0, 1)
                        for s in two:
                            pe.wait_ge(y_ready, ln + (2 * i + 1) * STREAMS + s + 1)
                            for j in range(HT):
                                nc.tensor.matmul(bank[s][j][:, :], wt("w1", i, j * P, P), y[s][:, :],
                                                 start=True, stop=True).then_inc(h_ready, 1)
                        for s in two:
                            for j in range(HT):
                                pe.wait_ge(hg_ready, ((trip * NB + i) * STREAMS + s) * HT + j + 1)
                                mm = nc.tensor.matmul(bank[s][0][:, :], wt("w2", i, j * P, P), h[s][:, j, :],
                                                      start=j == 0, stop=j == HT - 1)
                            mm.then_inc(f_ready, 1)
                        norm(2 * i + 2, lambda s: ga[s][:, :], 1, 2)

            @block.scalar
            def _(act):
                act.wait_ge(loaded, 16)
                with act.Fori(0, TRIPS) as trip:
                    ln = trip * (LN_PER_TRIP * STREAMS)

                    def norm(n, affine):
                        for s in two:
                            norm_act_square(nc, act, ns, ln + n * STREAMS + s + 1, cen[s][:, :], sq[s][:, :])
                        for s in two:
                            act.wait_ge(ns.normed_ready, ln + n * STREAMS + s + 1)
                            nc.scalar.activation(y[s][:, :], cen[s][:, :], ACT.Identity,
                                                 bias=affine if affine is not None else 0.0).then_inc(y_ready, 1)

                    norm(0, None)
                    for i in range(NB):
                        for s in two:
                            for j, (dst, bias) in enumerate(((eq, "bq"), (ek, "bk"))):
                                act.wait_ge(qkv_ready, ((trip * NB + i) * STREAMS + s) * 3 + j + 1)
                                nc.scalar.activation(dst[s][:, :], bank[s][j][:, :], ACT.Exp,
                                                     bias=wt(bias, i)).then_inc(exp_ready, 1)
                        for s in two:
                            n = (trip * NB + i) * STREAMS + s + 1
                            act.wait_ge(o_ready, n)
                            nc.scalar.activation(den[s][:, :], bank[s][3][:, :], ACT.Gelu_apprx_tanh,
                                                 bias=wt("bo", i)).then_inc(gelu1, 1)
                            act.wait_ge(gelu1, n)
                            nc.scalar.activation(ga[s][:, :], den[s][:, :], ACT.Gelu_apprx_tanh).then_inc(a_ready, 1)
                        norm(2 * i + 1, wt("c1", i))
                        for s in two:
                            for j in range(HT):
                                act.wait_ge(h_ready, ((trip * NB + i) * STREAMS + s) * HT + j + 1)
                                nc.scalar.activation(h[s][:, j, :], bank[s][j][:, :], ACT.Gelu_apprx_tanh,
                                                     bias=wt("b1", i, j, 1)).then_inc(hg_ready, 1)
                        for s in two:
                            act.wait_ge(f_ready, (trip * NB + i) * STREAMS + s + 1)
                            nc.scalar.activation(ga[s][:, :], bank[s][0][:, :], ACT.Gelu_apprx_tanh,
                                                 bias=wt("b2", i)).then_inc(a_ready, 1)
                        norm(2 * i + 2, wt("c2", i))

            @block.vector
            def _(dve):
                dve.wait_ge(loaded, 16)
                with dve.Fori(0, TRIPS) as trip:
                    ln = trip * (LN_PER_TRIP * STREAMS)
                    ch = Chain(dve, dve_step, trip, NB * STREAMS * 12)

                    def norm(n, src, m, v, gain, eps):
                        for s in two:
                            norm_dve_centre(nc, dve, ns, ln + n * STREAMS + s + 1, src(s), bank[s][m][:, :], cen[s][:, :])
                        for s in two:
                            norm_dve_vareps(nc, dve, ns, ln + n * STREAMS + s + 1, bank[s][v][:, :], vareps[s][:, :], eps)
                        for s in two:
                            norm_dve_scale(nc, dve, ns, ln + n * STREAMS + s + 1, cen[s][:, :], gain,
                                           bank[s][m][:, :], cen[s][:, :])

                    norm(0, lambda s: chunk_of(x, trip, s), 0, 1, 1.0, 1e-5)
                    for i in range(NB):
                        for s in two:
                            g = (trip * NB + i) * STREAMS + s
                            dve.wait_ge(exp_ready, g * 2 + 1)
                            a = ch.mark(nc.vector.tensor_scalar(qq[s][:, :], bank[s][0][:, :], wt("bq", i), 0.0, ALU.add, ALU.max))
                            dve.wait_ge(exp_ready, g * 2 + 2)
                            b = ch.mark(nc.vector.tensor_scalar(kk[s][:, :], bank[s][1][:, :], wt("bk", i), 0.0, ALU.add, ALU.max))
                            a = ch.mark(nc.vector.tensor_scalar(eq[s][:, :], eq[s][:, :], 1.0, -1.0, ALU.min, ALU.add))
                            b = ch.mark(nc.vector.tensor_scalar(ek[s][:, :], ek[s][:, :], 1.0, -1.0, ALU.min, ALU.add))
                            ch.wait(a)
                            ch.mark(nc.vector.scalar_tensor_tensor(qq[s][:, :], eq[s][:, :], 1.0, qq[s][:, :], ALU.add, ALU.add))
                            ch.wait(b)
                            kks, eks = seqs(kk[s][:, :]), seqs(ek[s][:, :])
                            for u in range(SEQ):
                                kd = ch.mark(nc.vector.scalar_tensor_tensor(
                                    kks[:, u, :], eks[:, u, :], 1.0, kks[:, u, :], ALU.add, ALU.add,
                                    accum_out=ksum[s][:, u:u + 1]))
                            ch.wait(kd)
                            dve.wait_ge(qkv_ready, g * 3 + 3)
                            for u in range(SEQ):
                                kvd = ch.mark(nc.vector.scalar_tensor_tensor(
                                    seqs(junk[s][:, :])[:, u, :], seqs(bank[s][2][:, :])[:, u, :], wt("bv", i),
                                    kks[:, u, :], ALU.add, ALU.mult, accum_out=kv[s][:, u:u + 1]))
                                dn = ch.mark(nc.vector.tensor_scalar(
                                    seqs(den[s][:, :])[:, u, :], seqs(qq[s][:, :])[:, u, :],
                                    ksum[s][:, u:u + 1], 1e-6, ALU.mult, ALU.add))
                            ch.wait(dn)
                            rc = ch.mark(nc.vector.reciprocal(junk[s][:, :], den[s][:, :]))
                            ch.wait(rc)
                            for u in range(SEQ):
                                vi = nc.vector.scalar_tensor_tensor(
                                    seqs(vv[s][:, :])[:, u, :], seqs(qq[s][:, :])[:, u, :], kv[s][:, u:u + 1],
                                    seqs(junk[s][:, :])[:, u, :], ALU.mult, ALU.mult)
                            vi.then_inc(v_ready, 1)
                        norm(2 * i + 1, lambda s: ga[s][:, :], 0, 1, wt("s1", i), 1e-6)
                        norm(2 * i + 2, lambda s: ga[s][:, :], 1, 2, wt("s2", i), 1e-6)
                    ch.close()

            @block.gpsimd
            def _(pool):
                pool.sem_inc(done, 1)
                with pool.Fori(0, TRIPS) as trip:
                    ln = trip * (LN_PER_TRIP * STREAMS)
                    for n in range(2 * NB + 1):
                        if n:
                            for s in two:
                                pool.wait_ge(a_ready, (trip * 2 * NB + n - 1) * STREAMS + s + 1)
                                nc.gpsimd.tensor_tensor(ga[s][:, :], ga[s][:, :], y[s][:, :], ALU.add).then_inc(t_ready, 1)
                        for s in two:
                            norm_pool_rstd(nc, pool, k, ns, ln + n * STREAMS + s + 1, vareps[s][:, :], rstd[s][:, :])
                    for s in two:
                        pool.wait_ge(y_ready, ln + 2 * NB * STREAMS + s + 1)
                        xs = chunk_of(x, trip, s)
                        nc.gpsimd.tensor_tensor(xs, xs, y[s][:, :], ALU.add).then_inc(done, 1)


def bcast(ap, axis, n):
    a = ap.unsqueeze(axis)
    shape = list(a.shape)
    shape[axis] = n
    return a.to_broadcast(shape)


def rank_by_value(nc, ch, k, vals, gt, eq, rank, tiles, n):
    other, own = bcast(vals, 2, n), bcast(vals, 3, n)
    ch.mark(nc.vector.tensor_tensor(gt, other, own, ALU.is_gt))
    e = ch.mark(nc.vector.tensor_tensor(eq, other, own, ALU.is_equal))
    ch.wait(e)
    e = ch.mark(nc.vector.tensor_tensor(eq, eq, bcast(k.lower[:, 0:n, 0:n], 1, tiles), ALU.mult))
    ch.wait(e)
    e = ch.mark(nc.vector.tensor_tensor(gt, gt, eq, ALU.add))
    ch.wait(e)
    return ch.mark(nc.vector.tensor_reduce(rank, gt, AX.X, ALU.add))


RANK_MARKS = 5


def l0_ffn(nc, k, w_dram, x):
    E, R, TOPK, SCALING = 8, 8, 2, 2.0
    ER = E * R
    with Stage(nc, "l0f") as st:
        w = st.sbuf("w", [P, w_dram.shape[1]])
        o = 0
        cuts = []
        for width in (P, ER, E, P, 1, E):
            cuts.append(w[:, o:o + width])
            o += width
        w_base, w_a, w_gate, w_b, bias, gate_b = cuts
        w_b = w_b[0:ER, :]
        two = range(STREAMS)
        cen = [st.sbuf(f"cen{s}", [P, C]) for s in two]
        sq = [st.sbuf(f"sq{s}", [P, C]) for s in two]
        n_ = [st.sbuf(f"n{s}", [P, C]) for s in two]
        vareps = [st.sbuf(f"vareps{s}", [P, TPC]) for s in two]
        rstd = [st.sbuf(f"rstd{s}", [P, TPC]) for s in two]
        lg = [st.sbuf(f"lg{s}", [P, TPC, E]) for s in two]
        ex = [st.sbuf(f"ex{s}", [P, TPC, E]) for s in two]
        rank = [st.sbuf(f"rank{s}", [P, TPC, E]) for s in two]
        gates = [st.sbuf(f"gates{s}", [P, TPC, E]) for s in two]
        gx = [st.sbuf(f"gx{s}", [P, TPC, E, R]) for s in two]
        gt = [st.sbuf(f"gt{s}", [P, TPC, E, E]) for s in two]
        eq = [st.sbuf(f"eq{s}", [P, TPC, E, E]) for s in two]
        top = [st.sbuf(f"top{s}", [P, TPC]) for s in two]
        xa = [st.sbuf(f"xa{s}", [ER, C]) for s in two]
        xg = [st.sbuf(f"xg{s}", [ER, C]) for s in two]
        bank = [[st.psum(f"ps{s}{j}", [P, C]) for j in range(4)] for s in two]
        loaded = st.sem("loaded")
        ns = NormSems(st)
        logits_ready = st.sem("logits_ready")
        xa_ready = st.sem("xa_ready")
        xa_copied = st.sem("xa_copied")
        shifted_ready = st.sem("shifted_ready")
        exp_ready = st.sem("exp_ready")
        gates_ready = st.sem("gates_ready")
        gspread_ready = st.sem("gspread_ready")
        xg_ready = st.sem("xg_ready")
        out_ready = st.sem("out_ready")
        dve_step = st.sem("dve_step")
        done = st.sem("done")

        with nc.Block() as block:

            @block.sync
            def _(sp):
                sp.dma_start(w[:, :], w_dram).then_inc(loaded, 16)

            @block.tensor
            def _(pe):
                pe.wait_ge(loaded, 16)
                with pe.Fori(0, TRIPS) as trip:
                    t2 = trip * STREAMS
                    pe.wait_ge(done, t2 + 1)
                    for s in two:
                        norm_pe_mean(nc, k, ns, chunk_of(x, trip, s), bank[s][0][:, :])
                    for s in two:
                        norm_pe_var(nc, pe, k, ns, t2 + s + 1, sq[s][:, :], bank[s][1][:, :])
                    for s in two:
                        norm_pe_spread(nc, pe, k, ns, t2 + s + 1, rstd[s][:, :], bank[s][0][:, :])
                    for s in two:
                        pe.wait_ge(ns.normed_ready, t2 + s + 1)
                        for t in range(TPC):
                            mm = nc.tensor.matmul(bank[s][1][:, t * E:(t + 1) * E], n_[s][:, t * P:(t + 1) * P],
                                                  w_gate, start=True, stop=True)
                        mm.then_inc(logits_ready, 1)
                        nc.tensor.matmul(bank[s][2][0:ER, :], w_a, n_[s][:, :], start=True, stop=True).then_inc(xa_ready, 1)
                    for s in two:
                        nc.tensor.matmul(bank[s][3][:, :], w_base, n_[s][:, :], start=True, stop=False)
                    for s in two:
                        pe.wait_ge(gates_ready, t2 + s + 1)
                        for t in range(TPC):
                            mm = nc.tensor.matmul(bank[s][0][0:ER, t * P:(t + 1) * P],
                                                  gx[s][:, t, :, :].rearrange("p e r -> p (e r)"),
                                                  k.ident[:, :], start=True, stop=True)
                        mm.then_inc(gspread_ready, 1)
                    for s in two:
                        pe.wait_ge(xg_ready, t2 + s + 1)
                        nc.tensor.matmul(bank[s][3][:, :], w_b, xg[s][:, :], start=False, stop=True).then_inc(out_ready, 1)

            @block.scalar
            def _(act):
                with act.Fori(0, TRIPS) as trip:
                    t2 = trip * STREAMS
                    for s in two:
                        norm_act_square(nc, act, ns, t2 + s + 1, cen[s][:, :], sq[s][:, :])
                    for s in two:
                        act.wait_ge(xa_ready, t2 + s + 1)
                        nc.scalar.activation(xa[s][:, :], bank[s][2][0:ER, :], ACT.Copy).then_inc(xa_copied, 1)
                    for s in two:
                        act.wait_ge(shifted_ready, t2 + s + 1)
                        nc.scalar.activation(ex[s][:, :, :], lg[s][:, :, :], ACT.Exp).then_inc(exp_ready, 1)

            @block.vector
            def _(dve):
                dve.sem_inc(done, 1)
                dve.wait_ge(loaded, 16)
                with dve.Fori(0, TRIPS) as trip:
                    t2 = trip * STREAMS
                    ch = Chain(dve, dve_step, trip, STREAMS * (RANK_MARKS + 6))
                    for s in two:
                        norm_dve_centre(nc, dve, ns, t2 + s + 1, chunk_of(x, trip, s), bank[s][0][:, :], cen[s][:, :])
                    for s in two:
                        norm_dve_vareps(nc, dve, ns, t2 + s + 1, bank[s][1][:, :], vareps[s][:, :], 1e-5)
                    for s in two:
                        norm_dve_scale(nc, dve, ns, t2 + s + 1, cen[s][:, :], 1.0, bank[s][0][:, :], n_[s][:, :])
                    for s in two:
                        dve.wait_ge(logits_ready, t2 + s + 1)
                        ps = bank[s][1][:, 0:TPC * E].rearrange("p (t e) -> p t e", e=E)
                        ch.wait(ch.mark(nc.vector.tensor_tensor(lg[s][:, :, :], ps, bcast(gate_b, 1, TPC), ALU.add)))
                        r = rank_by_value(nc, ch, k, lg[s][:, :, :], gt[s][:, :, :, :], eq[s][:, :, :, :],
                                          rank[s][:, :, :], TPC, E)
                        m = ch.mark(nc.vector.tensor_reduce(top[s][:, :], lg[s][:, :, :], AX.X, ALU.max))
                        ch.wait(m)
                        nc.vector.tensor_tensor(lg[s][:, :, :], lg[s][:, :, :], bcast(top[s][:, :], 2, E),
                                                ALU.subtract).then_inc(shifted_ready, 1)
                    for s in two:
                        dve.wait_ge(exp_ready, t2 + s + 1)
                        ch.wait(ch.mark(nc.vector.scalar_tensor_tensor(
                            gates[s][:, :, :], rank[s][:, :, :], float(TOPK), ex[s][:, :, :], ALU.is_lt, ALU.mult)))
                        ch.wait(ch.mark(nc.vector.tensor_reduce(top[s][:, :], gates[s][:, :, :], AX.X, ALU.add)))
                        ch.wait(ch.mark(nc.vector.reciprocal(top[s][:, :], top[s][:, :])))
                        ch.wait(ch.mark(nc.vector.scalar_tensor_tensor(
                            gates[s][:, :, :], gates[s][:, :, :], SCALING, bcast(top[s][:, :], 2, E), ALU.mult, ALU.mult)))
                        nc.vector.tensor_copy(gx[s][:, :, :, :], bcast(gates[s][:, :, :], 3, R)).then_inc(gates_ready, 1)
                    for s in two:
                        dve.wait_ge(gspread_ready, t2 + s + 1)
                        dve.wait_ge(xa_copied, t2 + s + 1)
                        nc.vector.tensor_tensor(xg[s][:, :], xa[s][:, :], bank[s][0][0:ER, :], ALU.mult).then_inc(xg_ready, 1)
                    for s in two:
                        dve.wait_ge(out_ready, t2 + s + 1)
                        xs = chunk_of(x, trip, s)
                        nc.vector.scalar_tensor_tensor(xs, bank[s][3][:, :], bias, xs, ALU.add, ALU.add).then_inc(done, 1)
                    ch.close()

            @block.gpsimd
            def _(pool):
                with pool.Fori(0, TRIPS) as trip:
                    for s in two:
                        norm_pool_rstd(nc, pool, k, ns, trip * STREAMS + s + 1, vareps[s][:, :], rstd[s][:, :])


BF16 = mybir.dt.bfloat16


def l1_attention(nc, k, w_dram, x):
    H, HD, EPS = 16, 8, 1.1920929e-07
    G, J, W = 4, 4, 32
    RING = 6
    UNITS = 12
    EVACS = 2 * G
    with Stage(nc, "l1a") as st:
        w = st.sbuf("w", [P, w_dram.shape[1]])
        cuts, o = {}, 0
        for name, rows, width in (("dq", 64, P), ("uq", 64, P), ("dkv", P, P), ("uk", P, P), ("kr", 64, P),
                                  ("qr", 64, P), ("uv", HD, P), ("o", HD, P), ("qw", P, 1), ("kw", P, 1)):
            cuts[name] = w[0:rows, o:o + width]
            o += width
        aq, ak, av, ar = (st.sbuf(n, [P, P]) for n in ("aq", "ak", "av", "ar"))
        uvo = st.sbuf("uvo", [P, P])
        block8 = st.sbuf("block8", [P, H, HD])
        mean8 = st.sbuf("mean8", [P, H])
        sel = st.sbuf("sel", [P, G, J, W])
        one_row = st.sbuf("one_row", [P, J])
        one_at8 = st.sbuf("one_at8", [P, 1])
        qscale = st.sbuf("qscale", [P, 1])
        identb = st.sbuf("identb", [P, P], BF16)
        mask = [st.sbuf(f"mask{i}", [P, 4, P], BF16) for i in range(2)]
        tick = st.sbuf("tick", [P, 1])
        cen, sq, n_ = st.sbuf("cen", [P, C]), st.sbuf("sq", [P, C]), st.sbuf("n", [P, C])
        vareps, rstd = st.sbuf("vareps", [P, TPC]), st.sbuf("rstd", [P, TPC])
        qc, kc, sqq, sqk = (st.sbuf(n, [P, C]) for n in ("qc", "kc", "sqq", "sqk"))
        mse = st.sbuf("mse", [P, 2 * TPC, H])
        rms = st.sbuf("rms", [P, 2 * TPC, H])
        half = st.sbuf("half", [P, 2 * TPC, H])
        rmsx = st.sbuf("rmsx", [P, 2 * TPC, H, HD])
        ke = st.sbuf("ke", [P, C])
        v9 = st.sbuf("v9", [P, TPC, H, HD + 1])
        kpad, qpad, qmax = (st.sbuf(n, [P, G, C]) for n in ("kpad", "qpad", "qmax"))
        mx = st.sbuf("mx", [P, TPC, H])
        negmax = st.sbuf("negmax", [P, TPC, G, J, W])
        probs = [st.sbuf(f"probs{b}", [P, UNITS, C]) for b in range(SEQ)]
        rsum = st.sbuf("rsum", [P, TPC, H])
        ctxn = st.sbuf("ctxn", [P, TPC, H, HD])
        bank = [st.psum(f"ps{j}", [P, C]) for j in range(8)]

        loaded, const_step, const_ready = st.sem("loaded"), st.sem("const_step"), st.sem("const_ready")
        folded_ps, folded = st.sem("folded_ps"), st.sem("folded")
        ns = NormSems(st)
        qkv_ready = st.sem("qkv_ready")
        qkv_copied = st.sem("qkv_copied")
        ms_ready = st.sem("ms_ready")
        mse_ready = st.sem("mse_ready")
        rms_ready = st.sem("rms_ready")
        rmsx_ready = st.sem("rmsx_ready")
        rspread_ready = st.sem("rspread_ready")
        qk_ready = st.sem("qk_ready")
        pad_ps = st.sem("pad_ps")
        pad_act = st.sem("pad_act")
        pad_dve = st.sem("pad_dve")
        score_ready = st.sem("score_ready")
        max_done = st.sem("max_done")
        negmax_ready = st.sem("negmax_ready")
        negT_ready = st.sem("negT_ready")
        qmax_ready = st.sem("qmax_ready")
        scoreT_ready = st.sem("scoreT_ready")
        exp_done = st.sem("exp_done")
        ticked = st.sem("ticked")
        masked = st.sem("masked")
        ctx_ready = st.sem("ctx_ready")
        ctxn_ready = st.sem("ctxn_ready")
        ctxT_ready = st.sem("ctxT_ready")
        dve_step = st.sem("dve_step")
        done = st.sem("done")

        ROUNDS_Q = [(1, 0, 2, 256), (1, 2, 2, 256), (0, 0, 4, 128)]
        ROUNDS_K = [(0, 0, 2, 256), (0, 2, 2, 256), (1, 0, 4, 128)]

        with nc.Block() as block:

            @block.sync
            def _(sp):
                sp.dma_start(w[:, :], w_dram).then_inc(loaded, 16)

            @block.gpsimd
            def _(pool):
                pool.sem_inc(ticked, 1)
                for m, v in ((block8, 1.0), (mean8, 1.0 / HD), (sel, 0.0), (one_row, 0.0), (v9, 1.0),
                             (negmax, 0.0), (mask[0], 0.0), (mask[1], 0.0), (half, -0.5)):
                    full = m[tuple(slice(None) for _ in m.shape)]
                    nc.gpsimd.memset(full, v).then_inc(const_step, 1)
                nc.gpsimd.tensor_copy(identb[:, :], k.ident[:, :]).then_inc(const_step, 1)
                pool.wait_ge(const_step, 10)

                def select(view, pattern, mult, base, op, fill, n):
                    nc.gpsimd.affine_select(out=view, in_=view, compare_op=op, fill=fill, base=base,
                                            pattern=pattern, channel_multiplier=mult).then_inc(const_step, 1)
                    pool.wait_ge(const_step, n)

                select(block8[:, :, :], [[-HD, H], [0, HD]], 1, 0, ALU.is_ge, 0.0, 11)
                select(block8[:, :, :], [[HD, H], [0, HD]], -1, HD - 1, ALU.is_ge, 0.0, 12)
                select(mean8[:, :], [[-HD, H]], 1, 0, ALU.is_ge, 0.0, 13)
                select(mean8[:, :], [[HD, H]], -1, HD - 1, ALU.is_ge, 0.0, 14)
                select(sel[:, :, :, 0:HD], [[-HD * J, G], [-HD, J], [-1, HD]], 1, 0, ALU.not_equal, 1.0, 15)
                select(one_row[:, :], [[-W, J]], 1, -HD, ALU.not_equal, 1.0, 16)
                select(mask[0][:, :, :], [[0, 4], [-1, P]], 1, 0, ALU.is_ge, -1e30, 17)
                for i, c in enumerate((1, 3)):
                    select(mask[1][:, c, :], [[-1, P]], 1, 0, ALU.is_ge, -1e30, 18 + i)
                nc.gpsimd.memset(cen[0:1, 0:1], 0.0).then_inc(const_ready, 1)
                with pool.Fori(0, NCH) as trip:
                    norm_pool_rstd(nc, pool, k, ns, trip + 1, vareps[:, :], rstd[:, :])
                    pool.wait_ge(mse_ready, trip + 1)
                    nc.gpsimd.tensor_tensor(rms[:, :, :], mse[:, :, :], half[:, :, :], ALU.pow).then_inc(rms_ready, 1)
                    for b in range(SEQ):
                        for u in range(UNITS):
                            _, _, g, _ = ROUNDS_K[u // J]
                            pool.wait_ge(exp_done, trip * (SEQ * UNITS) + b * UNITS + u + 1)
                            pr = probs[b][:, u, :].rearrange("p (g c) -> p g c", g=g)[:, :, 0:P]
                            pool.wait_ge(ticked, trip * (SEQ * UNITS) + b * UNITS + u + 1)
                            nc.gpsimd.tensor_tensor(tick[:, :], k.minus_half[:, 0:1], k.minus_half[:, 0:1],
                                                    ALU.add).then_inc(ticked, 1)
                            nc.gpsimd.affine_select(out=pr, in_=pr, compare_op=ALU.is_ge, fill=0.0, base=0,
                                                    pattern=[[0, g], [1, P]], channel_multiplier=-1).then_inc(masked, 1)

            @block.scalar
            def _(act):
                with act.Fori(0, NCH) as trip:
                    norm_act_square(nc, act, ns, trip + 1, cen[:, :], sq[:, :])
                    for j, (copy, square) in enumerate(((qc, sqq), (kc, sqk))):
                        act.wait_ge(qkv_ready, trip * 4 + j + 1)
                        nc.scalar.activation(square[:, :], bank[j][:, :], ACT.Square)
                        nc.scalar.activation(copy[:, :], bank[j][:, :], ACT.Copy).then_inc(qkv_copied, 1)
                    act.wait_ge(qkv_ready, trip * 4 + 4)
                    nc.scalar.activation(v9[:, :, :, 0:HD], bank[3][:, :].rearrange("p (t h d) -> p t h d", t=TPC, h=H),
                                         ACT.Copy).then_inc(qkv_copied, 1)
                    for i in range(0, EVACS, 2):
                        act.wait_ge(pad_ps, trip * EVACS + i + 1)
                        dst, bias = (kpad, one_at8[:, :]) if i < G else (qpad, 0.0)
                        nc.scalar.activation(dst[:, i % G, :], bank[PAD_BANK[i]][:, :], ACT.Identity,
                                             bias=bias).then_inc(pad_act, 1)
                    for b in range(SEQ):
                        for u in range(UNITS):
                            n = b * UNITS + u
                            act.wait_ge(scoreT_ready, trip * (SEQ * UNITS) + n + 1)
                            nc.scalar.activation(probs[b][:, u, :], bank[n % RING][:, :], ACT.Exp).then_inc(exp_done, 1)

            @block.vector
            def _(dve):
                dve.sem_inc(done, 1)
                dve.wait_ge(loaded, 16)
                dve.wait_ge(const_ready, 1)
                nc.vector.tensor_scalar(qscale[:, :], cuts["qw"], HD ** -0.5, None, ALU.mult)
                nc.vector.tensor_reduce(one_at8[:, :], one_row[:, :], AX.X, ALU.add)
                flat = block8[:, :, :].rearrange("p h d -> p (h d)")
                dve.wait_ge(folded_ps, 3)
                for m, b in ((aq, 0), (ak, 1), (ar, 2)):
                    nc.vector.tensor_tensor(m[:, :], bank[b][:, 0:P], flat, ALU.mult)
                dve.wait_ge(folded_ps, 4)
                nc.vector.tensor_copy(uvo[:, :], bank[3][:, 0:P]).then_inc(folded, 1)
                dve.wait_ge(folded_ps, 5)
                nc.vector.tensor_tensor(av[:, :], bank[4][:, 0:P], flat, ALU.mult).then_inc(folded, 1)
                with dve.Fori(0, NCH) as trip:
                    ch = Chain(dve, dve_step, trip, 1 + SEQ)
                    norm_dve_centre(nc, dve, ns, trip + 1, chunk_at(x, trip), bank[6][:, :], cen[:, :])
                    norm_dve_vareps(nc, dve, ns, trip + 1, bank[7][:, :], vareps[:, :], 1e-5)
                    norm_dve_scale(nc, dve, ns, trip + 1, cen[:, :], 1.0, bank[6][:, :], n_[:, :])
                    dve.wait_ge(ms_ready, trip + 1)
                    nc.vector.tensor_scalar(mse[:, :, :], bank[4][:, 0:2 * TPC * H].rearrange("p (t h) -> p t h", h=H),
                                            EPS, None, ALU.add).then_inc(mse_ready, 1)
                    dve.wait_ge(rms_ready, trip + 1)
                    nc.vector.tensor_copy(rmsx[:, :, :, :], bcast(rms[:, :, :], 3, HD)).then_inc(rmsx_ready, 1)
                    dve.wait_ge(rspread_ready, trip + 1)
                    a = ch.mark(nc.vector.scalar_tensor_tensor(ke[:, :], kc[:, :], cuts["kw"], bank[1][:, :],
                                                               ALU.mult, ALU.mult))
                    ch.wait(a)
                    nc.vector.tensor_tensor(ke[:, :], ke[:, :], bank[2][:, :], ALU.add).then_inc(qk_ready, 1)
                    nc.vector.scalar_tensor_tensor(qc[:, :], qc[:, :], qscale[:, :], bank[0][:, :],
                                                   ALU.mult, ALU.mult).then_inc(qk_ready, 1)
                    for i in range(1, EVACS, 2):
                        dve.wait_ge(pad_ps, trip * EVACS + i + 1)
                        if i < G:
                            op = nc.vector.tensor_scalar(kpad[:, i % G, :], bank[PAD_BANK[i]][:, :], one_at8[:, :],
                                                         None, ALU.add)
                        else:
                            op = nc.vector.tensor_copy(qpad[:, i % G, :], bank[PAD_BANK[i]][:, :])
                        op.then_inc(pad_dve, 1)
                    for b in range(SEQ):
                        for u in range(UNITS):
                            n = b * UNITS + u
                            qt, g0, g, cols = ROUNDS_Q[u // J]
                            dve.wait_ge(score_ready, trip * (SEQ * UNITS) + n + 1)
                            h0 = g0 * J + u % J
                            nc.vector.tensor_reduce(mx[:, b * 2 + qt, h0:h0 + (g - 1) * J + 1:J],
                                                    bank[n % RING][:, :].rearrange("p (g c) -> p g c", g=g),
                                                    AX.X, ALU.max).then_inc(max_done, 1)
                    dve.wait_ge(max_done, (trip + 1) * (SEQ * UNITS))
                    nc.vector.tensor_scalar(negmax[:, :, :, :, HD], mx[:, :, :].rearrange("p t (g j) -> p t g j", g=G),
                                            -1.0, None, ALU.mult).then_inc(negmax_ready, 1)
                    for g in range(G):
                        dve.wait_ge(negT_ready, trip * G + g + 1)
                        if g == 0:
                            dve.wait_ge(pad_act, (trip + 1) * (EVACS // 2))
                        nc.vector.tensor_tensor(qmax[:, g, :], qpad[:, g, :], bank[g][:, :], ALU.add).then_inc(qmax_ready, 1)
                    for b in range(SEQ):
                        dve.wait_ge(ctx_ready, trip * SEQ + b + 1)
                        cx = bank[6 + b][:, 0:2 * H * (HD + 1)].rearrange("p (t h d) -> p t h d", t=2, h=H)
                        a = ch.mark(nc.vector.reciprocal(rsum[:, 2 * b:2 * b + 2, :], cx[:, :, :, HD]))
                        ch.wait(a)
                        nc.vector.tensor_tensor(ctxn[:, 2 * b:2 * b + 2, :, :], cx[:, :, :, 0:HD],
                                                bcast(rsum[:, 2 * b:2 * b + 2, :], 3, HD), ALU.mult).then_inc(ctxn_ready, 1)
                    dve.wait_ge(ctxT_ready, trip + 1)
                    xs = chunk_at(x, trip)
                    nc.vector.tensor_tensor(xs, xs, bank[0][:, :], ALU.add).then_inc(done, 1)
                    ch.close()

            @block.tensor
            def _(pe):
                pe.wait_ge(loaded, 16)
                for b, (l, r) in enumerate((("dq", "uq"), ("dkv", "uk"), ("kr", "qr"), ("uv", "o"))):
                    nc.tensor.matmul(bank[b][:, 0:P], cuts[l], cuts[r], start=True, stop=True).then_inc(folded_ps, 1)
                pe.wait_ge(folded, 1)
                nc.tensor.matmul(bank[4][:, 0:P], cuts["dkv"], uvo[:, :], start=True, stop=True).then_inc(folded_ps, 1)
                pe.wait_ge(folded, 2)
                pe.wait_ge(const_ready, 1)
                with pe.Fori(0, NCH) as trip:
                    pe.wait_ge(done, trip + 1)
                    norm_pe_mean(nc, k, ns, chunk_at(x, trip), bank[6][:, :])
                    norm_pe_var(nc, pe, k, ns, trip + 1, sq[:, :], bank[7][:, :])
                    norm_pe_spread(nc, pe, k, ns, trip + 1, rstd[:, :], bank[6][:, :])
                    pe.wait_ge(ns.normed_ready, trip + 1)
                    for b, m in enumerate((aq, ak, ar)):
                        nc.tensor.matmul(bank[b][:, :], m[:, :], n_[:, :], start=True, stop=True).then_inc(qkv_ready, 1)
                    for t in range(TPC):
                        mm = nc.tensor.matmul(bank[3][:, t * P:(t + 1) * P], n_[:, t * P:(t + 1) * P], av[:, :],
                                              start=True, stop=True)
                    mm.then_inc(qkv_ready, 1)
                    for i, square in enumerate((sqq, sqk)):
                        pe.wait_ge(qkv_copied, trip * 3 + i + 1)
                        for t in range(TPC):
                            o = (i * TPC + t) * H
                            mm = nc.tensor.matmul(bank[4][:, o:o + H], square[:, t * P:(t + 1) * P], mean8[:, :],
                                                  start=True, stop=True)
                    mm.then_inc(ms_ready, 1)
                    pe.wait_ge(rmsx_ready, trip + 1)
                    for t in range(2 * TPC):
                        mm = nc.tensor.transpose(bank[t // TPC][:, t % TPC * P:(t % TPC + 1) * P],
                                                 rmsx[:, t, :, :].rearrange("p h d -> p (h d)"), k.ident[:, :])
                    mm.then_inc(rspread_ready, 1)
                    pe.wait_ge(qkv_copied, trip * 3 + 3)
                    for i in range(EVACS):
                        pe.wait_ge(qk_ready, trip * 2 + (1 if i < 3 else 2))
                        if i >= RING:
                            pe.wait_ge((pad_act, pad_dve)[i % 2], trip * (EVACS // 2) + (i - RING) // 2 + 1)
                        nc.tensor.matmul(bank[PAD_BANK[i]][:, :], sel[:, i % G, :, :].rearrange("p j w -> p (j w)"),
                                         (ke if i < G else qc)[:, :], start=True, stop=True).then_inc(pad_ps, 1)
                    pe.wait_ge(pad_act, (trip + 1) * (EVACS // 2))
                    pe.wait_ge(pad_dve, (trip + 1) * (EVACS // 2))
                    units = trip * (SEQ * UNITS)
                    for b in range(SEQ):
                        for r, (qt, g0, gn, cols) in enumerate(ROUNDS_Q):
                            for j in range(J):
                                n = b * UNITS + r * J + j
                                if n >= RING:
                                    pe.wait_ge(max_done, units + n - RING + 1)
                                nc.tensor.matmul(bank[n % RING][:, :], identb[:, :],
                                                 mask[qt][:, :, :].rearrange("p a c -> p (a c)"), start=True, stop=False)
                            for g in range(gn):
                                for j in range(J):
                                    n = b * UNITS + r * J + j
                                    rows, t0 = slice(W * j, W * j + W), b * S
                                    mm = nc.tensor.matmul(bank[n % RING][:, g * cols:(g + 1) * cols],
                                                          qpad[rows, g0 + g, t0 + qt * P:t0 + qt * P + P],
                                                          kpad[rows, g0 + g, t0:t0 + cols],
                                                          start=False, stop=g == gn - 1)
                                    if g == gn - 1:
                                        mm.then_inc(score_ready, 1)
                    pe.wait_ge(negmax_ready, trip + 1)
                    for g in range(G):
                        for t in range(TPC):
                            mm = nc.tensor.transpose(bank[g][:, t * P:(t + 1) * P],
                                                     negmax[:, t, g, :, :].rearrange("p j w -> p (j w)"), k.ident[:, :])
                        mm.then_inc(negT_ready, 1)
                    for b in range(SEQ):
                        for r, (kt, g0, gn, cols) in enumerate(ROUNDS_K):
                            for g in range(gn):
                                for j in range(J):
                                    n = b * UNITS + r * J + j
                                    rows, t0 = slice(W * j, W * j + W), b * S
                                    if g == 0 and n >= RING:
                                        pe.wait_ge(exp_done, units + n - RING + 1)
                                    elif g == 0:
                                        pe.wait_ge(qmax_ready, (trip + 1) * G)
                                    mm = nc.tensor.matmul(bank[n % RING][:, g * cols:(g + 1) * cols],
                                                          kpad[rows, g0 + g, t0 + kt * P:t0 + kt * P + P],
                                                          qmax[rows, g0 + g, t0 + kt * P:t0 + S],
                                                          start=True, stop=True)
                                    if g == gn - 1:
                                        mm.then_inc(scoreT_ready, 1)
                    for b in range(SEQ):
                        pe.wait_ge(masked, units + (b + 1) * UNITS)
                        for h in range(H):
                            g, j = h // J, h % J
                            first = probs[b][:, (g // 2) * J + j, (g % 2) * S:(g % 2 + 1) * S]
                            second = probs[b][:, 2 * J + j, g * P:(g + 1) * P]
                            o = h * (HD + 1)
                            nc.tensor.matmul(bank[6 + b][:, o:o + HD + 1], first[:, 0:P], v9[:, 2 * b, h, :],
                                             start=True, stop=True)
                            o += H * (HD + 1)
                            nc.tensor.matmul(bank[6 + b][:, o:o + HD + 1], first[:, P:S], v9[:, 2 * b, h, :],
                                             start=True, stop=False)
                            mm = nc.tensor.matmul(bank[6 + b][:, o:o + HD + 1], second, v9[:, 2 * b + 1, h, :],
                                                  start=False, stop=True)
                        mm.then_inc(ctx_ready, 1)
                    for b in range(SEQ):
                        pe.wait_ge(ctxn_ready, trip * SEQ + b + 1)
                        for t in (2 * b, 2 * b + 1):
                            mm = nc.tensor.transpose(bank[0][:, t * P:(t + 1) * P],
                                                     ctxn[:, t, :, :].rearrange("p h d -> p (h d)"), k.ident[:, :])
                    mm.then_inc(ctxT_ready, 1)


PAD_BANK = [3, 4, 5, 0, 1, 2, 3, 4]


def l1_ffn(nc, k, w_dram, x):
    E, F, FT = 8, 512, 4
    KEEP = 2 * TOK
    EX = E + 1
    TOP_BIT = 1 << 29
    BITS = 30
    N = E * NT
    with Stage(nc, "l1f") as st:
        w = st.sbuf("w", [P, w_dram.shape[1]])
        o = 0

        def cut(width, shape=None, **dims):
            nonlocal o
            a = w[:, o:o + width]
            o += width
            return a.rearrange(shape, **dims) if shape else a

        w_gate = cut(E)
        w1 = cut(EX * F, "p (e f) -> p e f", e=EX)
        w2 = cut(EX * F, "p (e t d) -> p e t d", e=EX, t=FT)
        b1 = cut(EX * FT, "p (e t) -> p e t", e=EX)
        b2 = cut(EX)
        n_all = st.sbuf("n_all", [P, TOK])
        two = range(STREAMS)
        cen = [st.sbuf(f"cen{s}", [P, C]) for s in two]
        sq = [st.sbuf(f"sq{s}", [P, C]) for s in two]
        nb = [st.sbuf(f"nb{s}", [P, C]) for s in two]
        vareps = [st.sbuf(f"vareps{s}", [P, TPC]) for s in two]
        rstd = [st.sbuf(f"rstd{s}", [P, TPC]) for s in two]
        lg = st.sbuf("lg", [P, NT, E])
        ex = st.sbuf("ex", [P, NT, E])
        tot = st.sbuf("tot", [P, NT])
        sc = st.sbuf("sc", [P, E, NT])
        junk = st.sbuf("junk", [P, N])
        bit, thr, cand, flag = (st.sbuf(n, [P, 1], I32) for n in ("bit", "thr", "cand", "flag"))
        cnt = st.sbuf("cnt", [P, 1])
        need = st.sbuf("need", [P, 1])
        ones = st.sbuf("ones", [P, P])
        before = st.sbuf("before", [P, P])
        gt, eq, colsum, pref = (st.sbuf(n, [P, N]) for n in ("gt", "eq", "colsum", "pref"))
        cum = [st.sbuf(f"cum{i}", [P, N]) for i in range(2)]
        gates = st.sbuf("gates", [P, NT, E])
        gch = [st.sbuf(f"gch{s}", [P, TPC, E]) for s in two]
        hg = st.sbuf("hg", [P, 2, FT, C])
        gs = st.sbuf("gs", [P, 2, C])
        wy = st.sbuf("wy", [P, 2, C])
        acc = st.sbuf("acc", [P, C])
        bank = [st.psum(f"ps{j}", [P, C]) for j in range(8)]

        loaded = st.sem("loaded")
        const_step = st.sem("const_step")
        ns = NormSems(st)
        copied = st.sem("copied")
        logits_ready = st.sem("logits_ready")
        logits_read = st.sem("logits_read")
        shifted_ready = st.sem("shifted")
        exp_ready = st.sem("exp_ready")
        count_ready = st.sem("count_ready")
        total_ready = st.sem("total_ready")
        eq_ready = st.sem("eq_ready")
        prefix_ready = st.sem("prefix_ready")
        gates_ready = st.sem("gates_ready")
        dve_step = st.sem("dve_step")
        gch_ready = st.sem("gch_ready")
        h_ready = st.sem("h_ready")
        hg_ready = st.sem("hg_ready")
        gspread_ready = st.sem("gspread")
        gs_ready = st.sem("gs_ready")
        y_ready = st.sem("y_ready")
        wy_ready = st.sem("wy_ready")
        acc_ready = st.sem("acc_ready")
        done = st.sem("done")

        with nc.Block() as block:

            @block.sync
            def _(sp):
                sp.dma_start(w[:, :], w_dram).then_inc(loaded, 16)

            @block.gpsimd
            def _(pool):
                pool.sem_inc(acc_ready, 1)
                nc.gpsimd.memset(ones[:, :], 1.0).then_inc(const_step, 1)
                nc.gpsimd.memset(before[:, :], 1.0).then_inc(const_step, 1)
                pool.wait_ge(const_step, 2)
                nc.gpsimd.affine_select(out=before[:, :], in_=before[:, :], compare_op=ALU.is_gt, fill=0.0,
                                        base=0, pattern=[[1, P]], channel_multiplier=-1).then_inc(const_step, 1)
                with pool.Fori(0, TRIPS) as trip:
                    for s in two:
                        norm_pool_rstd(nc, pool, k, ns, trip * STREAMS + s + 1, vareps[s][:, :], rstd[s][:, :])
                with pool.Fori(0, NCH) as trip:
                    for e in range(1, EX):
                        pool.wait_ge(wy_ready, trip * EX + e + 2)
                        if e == 1:
                            pool.wait_ge(done, trip + 1)
                            nc.gpsimd.tensor_tensor(acc[:, :], wy[:, 0, :], wy[:, 1, :], ALU.add).then_inc(acc_ready, 1)
                        else:
                            pool.wait_ge(acc_ready, trip * (EX - 1) + e)
                            nc.gpsimd.tensor_tensor(acc[:, :], acc[:, :], wy[:, e % 2, :], ALU.add).then_inc(acc_ready, 1)

            @block.scalar
            def _(act):
                act.wait_ge(loaded, 16)
                with act.Fori(0, TRIPS) as trip:
                    t2 = trip * STREAMS
                    for s in two:
                        norm_act_square(nc, act, ns, t2 + s + 1, cen[s][:, :], sq[s][:, :])
                    for s in two:
                        act.wait_ge(ns.normed_ready, t2 + s + 1)
                        nc.scalar.activation(chunk_of(n_all, trip, s), nb[s][:, :], ACT.Copy).then_inc(copied, 1)
                act.wait_ge(shifted_ready, 1)
                nc.scalar.activation(ex[:, :, :], lg[:, :, :], ACT.Exp).then_inc(exp_ready, 1)
                with act.Fori(0, NCH) as trip:
                    for e in range(EX):
                        if e < E:
                            act.wait_ge(gspread_ready, trip * E + e + 2)
                            if e >= 2:
                                act.wait_ge(wy_ready, trip * EX + e)
                            nc.scalar.activation(gs[:, e % 2, :], bank[6 + e % 2][:, :], ACT.Copy).then_inc(gs_ready, 1)
                        for j in range(FT):
                            act.wait_ge(h_ready, (trip * EX + e) * FT + j + 1)
                            if e >= 2 and j == 0:
                                act.wait_ge(y_ready, trip * EX + e - 1)
                            nc.scalar.activation(hg[:, e % 2, j, :], bank[j][:, :], ACT.Gelu_apprx_tanh,
                                                 bias=b1[:, e, j:j + 1]).then_inc(hg_ready, 1)

            @block.vector
            def _(dve):
                for one_ahead in (logits_read, wy_ready, done):
                    dve.sem_inc(one_ahead, 1)
                with dve.Fori(0, TRIPS) as trip:
                    t2 = trip * STREAMS
                    for s in two:
                        norm_dve_centre(nc, dve, ns, t2 + s + 1, chunk_of(x, trip, s), bank[s * 4][:, :], cen[s][:, :])
                    for s in two:
                        norm_dve_vareps(nc, dve, ns, t2 + s + 1, bank[s * 4 + 1][:, :], vareps[s][:, :], 1e-5)
                    for s in two:
                        norm_dve_scale(nc, dve, ns, t2 + s + 1, cen[s][:, :], 1.0, bank[s * 4][:, :], nb[s][:, :])
                    for s in two:
                        dve.wait_ge(logits_ready, t2 + s + 1)
                        nc.vector.tensor_copy(lg[:, bass.ds((t2 + s) * TPC, TPC), :],
                                              bank[s * 4 + 1][:, 0:TPC * E].rearrange("p (t e) -> p t e", e=E)).then_inc(logits_read, 1)
                ch = Chain(dve, dve_step, 0, 0)

                def step(op):
                    ch.wait(ch.mark(op))

                dve.wait_ge(logits_read, NCH + 1)
                step(nc.vector.tensor_reduce(tot[:, :], lg[:, :, :], AX.X, ALU.max))
                nc.vector.tensor_tensor(lg[:, :, :], lg[:, :, :], bcast(tot[:, :], 2, E), ALU.subtract).then_inc(shifted_ready, 1)
                dve.wait_ge(exp_ready, 1)
                step(nc.vector.tensor_reduce(tot[:, :], ex[:, :, :], AX.X, ALU.add))
                step(nc.vector.reciprocal(tot[:, :], tot[:, :]))
                step(nc.vector.tensor_tensor(sc[:, :, :].rearrange("p e t -> p t e"), ex[:, :, :],
                                             bcast(tot[:, :], 2, E), ALU.mult))
                step(nc.vector.memset(bit[:, :], TOP_BIT))
                step(nc.vector.memset(thr[:, :], 0))
                flat = sc[:, :, :].rearrange("p e t -> p (e t)")
                start = ch.n
                with dve.Fori(0, BITS) as trip:
                    c2 = Chain(dve, dve_step, trip, 5)
                    c2.base = trip * 5 + start
                    c2.wait(c2.mark(nc.vector.tensor_tensor(cand[:, :], thr[:, :], bit[:, :], ALU.bitwise_or)))
                    nc.vector.tensor_scalar(junk[:, :], flat, cand[:, :].bitcast(FP32), 0.0, ALU.is_ge, ALU.add,
                                            accum_out=cnt[:, :]).then_inc(count_ready, 1)
                    dve.wait_ge(total_ready, trip + 1)
                    c2.wait(c2.mark(nc.vector.tensor_scalar(flag[:, :], bank[0][:, 0:1], float(KEEP), -1.0, ALU.is_ge, ALU.mult)))
                    c2.wait(c2.mark(nc.vector.tensor_tensor(cand[:, :], cand[:, :], flag[:, :], ALU.bitwise_and)))
                    c2.wait(c2.mark(nc.vector.tensor_tensor(thr[:, :], thr[:, :], cand[:, :], ALU.bitwise_or)))
                    c2.wait(c2.mark(nc.vector.tensor_scalar(bit[:, :], bit[:, :], 1, None, ALU.logical_shift_right)))
                    c2.close()
                ch.n = start + 5 * BITS
                tf = thr[:, :].bitcast(FP32)
                dve.wait_ge(count_ready, BITS)
                nc.vector.tensor_scalar(gt[:, :], flat, tf, 0.0, ALU.is_gt, ALU.add, accum_out=cnt[:, :]).then_inc(count_ready, 1)
                nc.vector.tensor_scalar(eq[:, :], flat, tf, None, ALU.is_equal).then_inc(eq_ready, 1)
                dve.wait_ge(total_ready, BITS + 1)
                step(nc.vector.tensor_scalar(need[:, :], bank[0][:, 0:1], -1.0, float(KEEP), ALU.mult, ALU.add))
                dve.wait_ge(prefix_ready, 1)
                nc.vector.tensor_copy(pref[:, :], bank[2][:, :])
                nc.vector.tensor_copy(colsum[:, :], bank[1][:, :])
                step(nc.vector.tensor_copy(cum[0][:, :], bank[1][:, :]))
                i, d = 0, 1
                while d < N:
                    a, b = cum[i], cum[1 - i]
                    ch.mark(nc.vector.tensor_copy(b[:, 0:d], a[:, 0:d]))
                    step(nc.vector.tensor_tensor(b[:, d:N], a[:, d:N], a[:, 0:N - d], ALU.add))
                    i, d = 1 - i, 2 * d
                step(nc.vector.tensor_tensor(pref[:, :], pref[:, :], cum[i][:, :], ALU.add))
                step(nc.vector.tensor_tensor(pref[:, :], pref[:, :], colsum[:, :], ALU.subtract))
                step(nc.vector.scalar_tensor_tensor(pref[:, :], pref[:, :], need[:, :], eq[:, :], ALU.is_lt, ALU.mult))
                step(nc.vector.tensor_tensor(pref[:, :], pref[:, :], gt[:, :], ALU.add))
                step(nc.vector.tensor_tensor(gates[:, :, :].rearrange("p t e -> p e t"), sc[:, :, :],
                                             pref[:, :].rearrange("p (e t) -> p e t", e=E), ALU.mult))
                with dve.Fori(0, NCH) as trip:
                    if True:
                        dve.wait_ge(gspread_ready, trip * E + 1)
                        nc.vector.tensor_copy(gch[0][:, :, :], gates[:, bass.ds(trip * TPC, TPC), :]).then_inc(gch_ready, 1)
                    for e in range(EX):
                        dve.wait_ge(y_ready, trip * EX + e + 1)
                        if e >= 2:
                            dve.wait_ge(acc_ready, trip * (EX - 1) + e)
                        else:
                            dve.wait_ge(done, trip + 1)
                        if e < E:
                            dve.wait_ge(gs_ready, trip * E + e + 1)
                            op = nc.vector.scalar_tensor_tensor(wy[:, e % 2, :], bank[4 + e % 2][:, :], b2[:, e:e + 1],
                                                                gs[:, e % 2, :], ALU.add, ALU.mult)
                        else:
                            op = nc.vector.tensor_scalar(wy[:, e % 2, :], bank[4 + e % 2][:, :], b2[:, e:e + 1], None, ALU.add)
                        op.then_inc(wy_ready, 1)
                    dve.wait_ge(acc_ready, (trip + 1) * (EX - 1) + 1)
                    xs = chunk_at(x, trip)
                    nc.vector.tensor_tensor(xs, xs, acc[:, :], ALU.add).then_inc(done, 1)

            @block.tensor
            def _(pe):
                pe.sem_inc(gspread_ready, 1)
                pe.wait_ge(loaded, 16)
                with pe.Fori(0, TRIPS) as trip:
                    t2 = trip * STREAMS
                    pe.wait_ge(logits_read, t2 + 1)
                    for s in two:
                        norm_pe_mean(nc, k, ns, chunk_of(x, trip, s), bank[s * 4][:, :])
                    for s in two:
                        norm_pe_var(nc, pe, k, ns, t2 + s + 1, sq[s][:, :], bank[s * 4 + 1][:, :])
                    for s in two:
                        norm_pe_spread(nc, pe, k, ns, t2 + s + 1, rstd[s][:, :], bank[s * 4][:, :])
                    for s in two:
                        pe.wait_ge(copied, t2 + s + 1)
                        for t in range(TPC):
                            mm = nc.tensor.matmul(bank[s * 4 + 1][:, t * E:(t + 1) * E], nb[s][:, t * P:(t + 1) * P],
                                                  w_gate, start=True, stop=True)
                        mm.then_inc(logits_ready, 1)
                pe.wait_ge(const_step, 3)
                pe.wait_ge(logits_read, NCH + 1)
                with pe.Fori(0, BITS + 1) as trip:
                    pe.wait_ge(count_ready, trip + 1)
                    nc.tensor.matmul(bank[0][:, 0:1], ones[:, :], cnt[:, :], start=True, stop=True).then_inc(total_ready, 1)
                pe.wait_ge(eq_ready, 1)
                nc.tensor.matmul(bank[1][:, :], ones[:, :], eq[:, :], start=True, stop=True)
                nc.tensor.matmul(bank[2][:, :], before[:, :], eq[:, :], start=True, stop=True).then_inc(prefix_ready, 1)
                pe.wait_ge(gch_ready, 1)

                with pe.Fori(0, NCH) as trip:
                    def inner(e):
                        for j in range(FT):
                            if e:
                                pe.wait_ge(hg_ready, (trip * EX + e - 1) * FT + j + 1)
                            nc.tensor.matmul(bank[j][:, :], w1[:, e, j * P:(j + 1) * P], chunk_at(n_all, trip),
                                             start=True, stop=True).then_inc(h_ready, 1)

                    pe.wait_ge(wy_ready, trip * EX + 1)
                    inner(0)
                    for e in range(EX):
                        if e < E:
                            if e >= 2:
                                pe.wait_ge(gs_ready, trip * E + e - 1)
                            else:
                                pe.wait_ge(gch_ready, trip + 1)
                            for t in range(TPC):
                                mm = nc.tensor.transpose(bank[6 + e % 2][:, t * P:(t + 1) * P],
                                                         gch[0][:, t, e:e + 1].to_broadcast([P, P]), k.ident[:, :])
                            mm.then_inc(gspread_ready, 1)
                        if e + 1 < EX:
                            inner(e + 1)
                        if e >= 2:
                            pe.wait_ge(wy_ready, trip * EX + e)
                        pe.wait_ge(hg_ready, (trip * EX + e) * FT + FT)
                        for j in range(FT):
                            mm = nc.tensor.matmul(bank[4 + e % 2][:, :], w2[:, e, j, :], hg[:, e % 2, j, :],
                                                  start=j == 0, stop=j == FT - 1)
                        mm.then_inc(y_ready, 1)


class RmsSems:

    def __init__(self, st, name):
        self.square_ready = st.sem(name + "_square_ready")
        self.ms_ready = st.sem(name + "_ms_ready")
        self.mseps_ready = st.sem(name + "_mseps_ready")
        self.rms_ready = st.sem(name + "_rms_ready")
        self.spread_ready = st.sem(name + "_spread_ready")
        self.normed_ready = st.sem(name + "_normed_ready")


def l2_attention(nc, k, w_dram, x):
    H, HD, F, FT = 16, 8, 512, 4
    EPS = 1e-6
    BG, BL = 8, 4
    with ExitStack() as outer:
        w = outer.enter_context(nc.sbuf_tensor("l2a_w", [P, w_dram.shape[1]], FP32))
        n_all = outer.enter_context(nc.sbuf_tensor("l2a_n_all", [P, TOK], FP32))
        scratch = {n: nc.dram_tensor(f"l2a_{n}_scratch", (P, TOK), FP32).ap() for n in ("q", "k", "v", "o")}
        beta_dram = nc.dram_tensor("l2a_beta_scratch", (H, TOK), FP32).ap()
        cuts, o = {}, 0
        for name, width in (("wq", P), ("wk", P), ("wv", P), ("wb", H), ("wo", P), ("wg", F), ("wu", F),
                            ("wd", F), ("ln1", 1), ("ln2", 1)):
            cuts[name] = w[:, o:o + width]
            o += width
        l2_project(nc, k, w_dram, x, w, cuts, n_all, scratch, beta_dram, H, HD, EPS)
        l2_recurrence(nc, k, scratch, beta_dram, H, HD, BG, BL)
        l2_output(nc, k, x, cuts, n_all, scratch["o"], FT, EPS)


def l2_project(nc, k, w_dram, x, w, cuts, n_all, scratch, beta_dram, H, HD, EPS):
    with Stage(nc, "l2p") as st:
        two = range(STREAMS)
        heads = st.sbuf("heads", [P, HD, H])
        headsum = st.sbuf("headsum", [P, H])
        half = st.sbuf("half", [P, 2 * TPC, H])
        cen = [st.sbuf(f"cen{s}", [P, C]) for s in two]
        sq = [st.sbuf(f"sq{s}", [P, C]) for s in two]
        nb = [st.sbuf(f"nb{s}", [P, C]) for s in two]
        xr = [st.sbuf(f"xr{s}", [P, C]) for s in two]
        vareps = [st.sbuf(f"vareps{s}", [P, TPC]) for s in two]
        rstd = [st.sbuf(f"rstd{s}", [P, TPC]) for s in two]
        qkv = [[st.sbuf(f"{n}{s}", [P, C]) for s in two] for n in ("q", "k", "v")]
        sqq, sqk = ([st.sbuf(f"{n}{s}", [P, C]) for s in two] for n in ("sqq", "sqk"))
        beta = [st.sbuf(f"beta{s}", [H, C]) for s in two]
        mse, rms = ([st.sbuf(f"{n}{s}", [P, 2 * TPC, H]) for s in two] for n in ("mse", "rms"))
        rmsx = [st.sbuf(f"rmsx{s}", [P, 2 * TPC, HD, H]) for s in two]
        bank = [[st.psum(f"ps{s}{j}", [P, C]) for j in range(4)] for s in two]
        loaded, const_step = st.sem("loaded"), st.sem("const_step")
        ns, rs = NormSems(st), RmsSems(st, "rms")
        n_copied = st.sem("n_copied")
        proj_ready = st.sem("proj_ready")
        act_ready = st.sem("act_ready")
        sq_ready = st.sem("sq_ready")
        beta_ready = st.sem("beta_ready")
        ss_ready = st.sem("ss_ready")
        sseps_ready = st.sem("sseps_ready")
        l2_ready = st.sem("l2_ready")
        l2x_ready = st.sem("l2x_ready")
        l2spread_ready = st.sem("l2spread")
        qk_ready = st.sem("qk_ready")
        stored = st.sem_each("stored")
        dve_step = st.sem("dve_step")

        with nc.Block() as block:

            @block.sync
            def _(sp):
                for s in two:
                    sp.sem_inc(stored[s], 1)
                sp.dma_start(w[:, :], w_dram).then_inc(loaded, 16)
                with sp.Fori(0, TRIPS) as trip:
                    for s in two:
                        at = bass.ds((trip * STREAMS + s) * C, C)
                        sp.wait_ge(act_ready, (trip * STREAMS + s) * 4 + 3)
                        sp.dma_start(scratch["v"][:, at], qkv[2][s][:, :]).then_inc(stored[s], 16)
                        sp.wait_ge(beta_ready, trip * STREAMS + s + 1)
                        sp.dma_start(beta_dram[:, at], beta[s][:, :]).then_inc(stored[s], 16)
                    for s in two:
                        at = bass.ds((trip * STREAMS + s) * C, C)
                        sp.wait_ge(qk_ready, (trip * STREAMS + s) * 2 + 3)
                        sp.dma_start(scratch["q"][:, at], qkv[0][s][:, :]).then_inc(stored[s], 16)
                        sp.dma_start(scratch["k"][:, at], qkv[1][s][:, :]).then_inc(stored[s], 16)
                for s in two:
                    sp.wait_ge(stored[s], TRIPS * 64 + 1)

            @block.gpsimd
            def _(pool):
                nc.gpsimd.memset(heads[:, :, :], 0.0).then_inc(const_step, 1)
                nc.gpsimd.memset(half[:, :, :], -0.5).then_inc(const_step, 1)
                pool.wait_ge(const_step, 2)
                nc.gpsimd.affine_select(out=heads[:, :, :], in_=heads[:, :, :], compare_op=ALU.not_equal, fill=1.0,
                                        base=0, pattern=[[-H, HD], [-1, H]], channel_multiplier=1).then_inc(const_step, 1)
                with pool.Fori(0, TRIPS) as trip:
                    t2 = trip * STREAMS
                    for s in two:
                        norm_pool_rstd(nc, pool, k, ns, t2 + s + 1, vareps[s][:, :], rstd[s][:, :])
                    for s in two:
                        pool.wait_ge(rs.mseps_ready, t2 + s + 1)
                        nc.gpsimd.tensor_tensor(rstd[s][:, :], vareps[s][:, :], k.minus_half[:, 0:TPC], ALU.pow).then_inc(rs.rms_ready, 1)
                    for s in two:
                        pool.wait_ge(sseps_ready, t2 + s + 1)
                        nc.gpsimd.tensor_tensor(rms[s][:, :, :], mse[s][:, :, :], half[:, :, :], ALU.pow).then_inc(l2_ready, 1)

            @block.scalar
            def _(act):
                with act.Fori(0, TRIPS) as trip:
                    t2 = trip * STREAMS
                    for s in two:
                        norm_act_square(nc, act, ns, t2 + s + 1, cen[s][:, :], sq[s][:, :])
                    for s in two:
                        act.wait_ge(ns.normed_ready, t2 + s + 1)
                        nc.scalar.activation(sq[s][:, :], nb[s][:, :], ACT.Square).then_inc(rs.square_ready, 1)
                        nc.scalar.activation(chunk_of(n_all, trip, s), nb[s][:, :], ACT.Copy).then_inc(n_copied, 1)
                    for s in two:
                        for j in (2, 1, 0):
                            act.wait_ge(proj_ready, (t2 + s) * 4 + 3 - j)
                            if j == 2:
                                act.wait_ge(stored[s], trip * 64 + 1)
                            nc.scalar.activation(qkv[j][s][:, :], bank[s][j][:, :], ACT.Silu).then_inc(act_ready, 1)
                        act.wait_ge(proj_ready, (t2 + s) * 4 + 4)
                        nc.scalar.activation(beta[s][:, :], bank[s][3][0:H, :], ACT.Tanh, scale=0.5).then_inc(act_ready, 1)
                        for j, square in ((1, sqk), (0, sqq)):
                            act.wait_ge(act_ready, (t2 + s) * 4 + 3 - j)
                            nc.scalar.activation(square[s][:, :], qkv[j][s][:, :], ACT.Square).then_inc(sq_ready, 1)

            @block.vector
            def _(dve):
                dve.wait_ge(loaded, 16)
                dve.wait_ge(const_step, 3)
                nc.vector.tensor_reduce(headsum[:, :], heads[:, :, :].rearrange("p d h -> p h d"), AX.X, ALU.add).then_inc(dve_step, 1)
                with dve.Fori(0, TRIPS) as trip:
                    t2 = trip * STREAMS
                    for s in two:
                        norm_dve_centre(nc, dve, ns, t2 + s + 1, chunk_of(x, trip, s), bank[s][0][:, :], cen[s][:, :])
                    for s in two:
                        norm_dve_vareps(nc, dve, ns, t2 + s + 1, bank[s][1][:, :], vareps[s][:, :], 1e-5)
                    for s in two:
                        norm_dve_scale(nc, dve, ns, t2 + s + 1, cen[s][:, :], 1.0, bank[s][0][:, :], nb[s][:, :])
                    for s in two:
                        dve.wait_ge(rs.ms_ready, t2 + s + 1)
                        nc.vector.tensor_scalar(vareps[s][:, :], bank[s][1][:, 0:TPC], EPS, None, ALU.add).then_inc(rs.mseps_ready, 1)
                    for s in two:
                        dve.wait_ge(rs.spread_ready, t2 + s + 1)
                        nc.vector.scalar_tensor_tensor(xr[s][:, :], nb[s][:, :], cuts["ln1"], bank[s][0][:, :],
                                                       ALU.mult, ALU.mult).then_inc(rs.normed_ready, 1)
                    for s in two:
                        dve.wait_ge(act_ready, (t2 + s) * 4 + 4)
                        nc.vector.tensor_scalar(beta[s][:, :], beta[s][:, :], 0.5, 0.5, ALU.mult, ALU.add).then_inc(beta_ready, 1)
                    for s in two:
                        dve.wait_ge(ss_ready, t2 + s + 1)
                        nc.vector.tensor_scalar(mse[s][:, :, :], bank[s][2][:, 0:2 * TPC * H].rearrange("p (t h) -> p t h", h=H),
                                                EPS, None, ALU.add).then_inc(sseps_ready, 1)
                    for s in two:
                        dve.wait_ge(l2_ready, t2 + s + 1)
                        nc.vector.tensor_copy(rmsx[s][:, :, :, :], bcast(rms[s][:, :, :], 2, HD)).then_inc(l2x_ready, 1)
                    for s in two:
                        dve.wait_ge(l2spread_ready, t2 + s + 1)
                        for j in (0, 1):
                            q = qkv[j][s]
                            nc.vector.tensor_tensor(q[:, :], q[:, :], bank[s][j][:, :], ALU.mult).then_inc(qk_ready, 1)

            @block.tensor
            def _(pe):
                pe.sem_inc(qk_ready, 1)
                pe.wait_ge(loaded, 16)
                pe.wait_ge(dve_step, 1)
                with pe.Fori(0, TRIPS) as trip:
                    t2 = trip * STREAMS
                    pe.wait_ge(qk_ready, t2 * 2 + 1)
                    for s in two:
                        norm_pe_mean(nc, k, ns, chunk_of(x, trip, s), bank[s][0][:, :])
                    for s in two:
                        norm_pe_var(nc, pe, k, ns, t2 + s + 1, sq[s][:, :], bank[s][1][:, :])
                    for s in two:
                        norm_pe_spread(nc, pe, k, ns, t2 + s + 1, rstd[s][:, :], bank[s][0][:, :])
                    for s in two:
                        pe.wait_ge(rs.square_ready, t2 + s + 1)
                        for t in range(TPC):
                            mm = nc.tensor.matmul(bank[s][1][:, t:t + 1], sq[s][:, t * P:(t + 1) * P], k.mean[:, 0:1],
                                                  start=True, stop=True)
                        mm.then_inc(rs.ms_ready, 1)
                    for s in two:
                        pe.wait_ge(rs.rms_ready, t2 + s + 1)
                        for t in range(TPC):
                            mm = nc.tensor.transpose(bank[s][0][:, t * P:(t + 1) * P],
                                                     rstd[s][:, t:t + 1].to_broadcast([P, P]), k.ident[:, :])
                        mm.then_inc(rs.spread_ready, 1)
                    for s in two:
                        pe.wait_ge(rs.normed_ready, t2 + s + 1)
                        for j, name in ((2, "wv"), (1, "wk"), (0, "wq")):
                            nc.tensor.matmul(bank[s][j][:, :], cuts[name], xr[s][:, :], start=True, stop=True).then_inc(proj_ready, 1)
                        nc.tensor.matmul(bank[s][3][0:H, :], cuts["wb"], xr[s][:, :], start=True, stop=True).then_inc(proj_ready, 1)
                    for s in two:
                        for i, (j, square) in enumerate(((1, sqk), (0, sqq))):
                            pe.wait_ge(sq_ready, (t2 + s) * 2 + i + 1)
                            for t in range(TPC):
                                o = (j * TPC + t) * H
                                mm = nc.tensor.matmul(bank[s][2][:, o:o + H], square[s][:, t * P:(t + 1) * P], headsum[:, :],
                                                      start=True, stop=True)
                        mm.then_inc(ss_ready, 1)
                    for s in two:
                        pe.wait_ge(l2x_ready, t2 + s + 1)
                        for t in range(2 * TPC):
                            mm = nc.tensor.transpose(bank[s][t // TPC][:, t % TPC * P:(t % TPC + 1) * P],
                                                     rmsx[s][:, t, :, :].rearrange("p d h -> p (d h)"), k.ident[:, :])
                        mm.then_inc(l2spread_ready, 1)


def l2_recurrence(nc, k, scratch, beta_dram, H, HD, BG, BL):
    STEPS = 4
    RING = 2 * STEPS
    SV = BL * HD
    SS = SV * HD
    with Stage(nc, "l2r") as st:
        q, kk, v = (st.sbuf(n, [P, HD, BL, S]) for n in ("q", "k", "v"))
        beta = st.sbuf("beta", [P, BL, S])
        states = st.sbuf("states", [P, RING, BL, HD, HD])
        prod = st.sbuf("prod", [P, BL, HD, HD])
        upd = st.sbuf("upd", [P, BL, HD, HD])
        seen = st.sbuf("seen", [P, BL, HD])
        delta = st.sbuf("delta", [P, BL, HD])
        pq = st.sbuf("pq", [P, STEPS * SV, HD])
        tick = st.sbuf("tick", [P, 1])
        k_half = k.minus_half[:, 0:1]
        loaded = [st.sem(f"loaded_{n}") for n in ("k", "v", "q", "beta")]
        stored = st.sem("stored")
        dve_step = st.sem("dve_step")
        state_ready = st.sem("state_ready")
        products = st.sem("products")
        pool_step = st.sem("pool_step")
        out_ready = st.sem("out_ready")

        def by_dim(name, d):
            return scratch[name][d * H:(d + 1) * H, :].rearrange("h (g n) -> (h g) n", g=BG)

        with nc.Block() as block:

            @block.sync
            def _(sp):
                sp.dma_start(beta[:, :, :].rearrange("p b t -> p (b t)"),
                             beta_dram.rearrange("h (g n) -> (h g) n", g=BG)).then_inc(loaded[3], 16)
                for n, (name, dst) in enumerate((("k", kk), ("v", v), ("q", q))):
                    for d in range(HD):
                        sp.dma_start(dst[:, d, :, :].rearrange("p b t -> p (b t)"), by_dim(name, d)).then_inc(loaded[n], 16)
                sp.wait_ge(out_ready, S // STEPS + 1)
                for d in range(HD):
                    sp.dma_start(by_dim("o", d), q[:, d, :, :].rearrange("p b t -> p (b t)")).then_inc(stored, 16)
                sp.wait_ge(stored, HD * 16)

            @block.vector
            def _(dve):
                nc.vector.memset(states[:, RING - 1, :, :, :], 0.0).then_inc(state_ready, 1)
                for n in (0, 1):
                    dve.wait_ge(loaded[n], HD * 16)
                dve.wait_ge(loaded[3], 16)
                with dve.Fori(0, S // RING) as trip:
                    ch = Chain(dve, dve_step, trip, RING * 5)
                    for i in range(RING):
                        t = trip * RING + i
                        at = bass.ds(t, 1)
                        kt = kk[:, :, :, at].rearrange("p d b t -> p b (d t)")
                        vt = v[:, :, :, at].rearrange("p d b t -> p b (d t)")
                        bt = beta[:, :, at]
                        old, new = states[:, (i - 1) % RING, :, :, :], states[:, i, :, :, :]
                        kb = bcast(kt, 2, HD)
                        dve.wait_ge(state_ready, t + 1)
                        ch.wait(ch.mark(nc.vector.tensor_tensor(prod[:, :, :, :], old, kb, ALU.mult)))
                        ch.wait(ch.mark(nc.vector.tensor_reduce(seen[:, :, :], prod[:, :, :, :], AX.X, ALU.add)))
                        ch.wait(ch.mark(nc.vector.tensor_tensor(delta[:, :, :], vt, seen[:, :, :], ALU.subtract)))
                        ch.wait(ch.mark(nc.vector.tensor_tensor(delta[:, :, :], delta[:, :, :],
                                                                bt.to_broadcast([P, BL, HD]), ALU.mult)))
                        ch.wait(ch.mark(nc.vector.tensor_tensor(upd[:, :, :, :], bcast(delta[:, :, :], 3, HD), kb, ALU.mult)))
                        if i % STEPS == 0:
                            dve.wait_ge(products, trip * 2 + i // STEPS + 1)
                        nc.vector.tensor_tensor(new, old, upd[:, :, :, :], ALU.add).then_inc(state_ready, 1)
                    ch.close()

            @block.gpsimd
            def _(pool):
                pool.sem_inc(products, 2)
                pool.sem_inc(out_ready, 1)
                pool.wait_ge(loaded[2], HD * 16)
                with pool.Fori(0, S // RING) as trip:
                    ch = Chain(pool, pool_step, trip, 2 * 4)
                    for half in range(2):
                        t0 = trip * RING + half * STEPS
                        pool.wait_ge(out_ready, trip * 2 + half + 1)
                        pool.wait_ge(state_ready, t0 + STEPS + 1)
                        ch.mark(nc.gpsimd.tensor_tensor(tick[:, :], k_half, k_half, ALU.add))
                        for m in range(STEPS):
                            qt = bcast(q[:, :, :, bass.ds(t0 + m, 1)].rearrange("p d b t -> p b (d t)"), 2, HD)
                            last = nc.gpsimd.tensor_tensor(
                                pq[:, m * SV:(m + 1) * SV, :].rearrange("p (b v) k -> p b v k", b=BL),
                                states[:, half * STEPS + m, :, :, :], qt, ALU.mult)
                        last.then_inc(products, 1)
                        pool.wait_ge(products, trip * 2 + half + 3)
                        ch.wait(ch.mark(nc.gpsimd.tensor_tensor(pq[:, :, 0:4], pq[:, :, 0:4], pq[:, :, 4:8], ALU.add)))
                        ch.wait(ch.mark(nc.gpsimd.tensor_tensor(pq[:, :, 0:2], pq[:, :, 0:2], pq[:, :, 2:4], ALU.add)))
                        ch.mark(nc.gpsimd.tensor_tensor(tick[:, :], k_half, k_half, ALU.add))
                        nc.gpsimd.tensor_tensor(q[:, :, :, bass.ds(t0, STEPS)].rearrange("p d b t -> p t b d"),
                                                pq[:, :, 0].rearrange("p (t b v) -> p t b v", t=STEPS, b=BL),
                                                pq[:, :, 1].rearrange("p (t b v) -> p t b v", t=STEPS, b=BL),
                                                ALU.add).then_inc(out_ready, 1)
                    ch.close()


def l2_output(nc, k, x, cuts, n_all, o_dram, FT, EPS):
    with Stage(nc, "l2o") as st:
        two = range(STREAMS)
        o = [st.sbuf(f"o{s}", [P, C]) for s in two]
        h = [st.sbuf(f"h{s}", [P, C]) for s in two]
        sq = [st.sbuf(f"sq{s}", [P, C]) for s in two]
        y = [st.sbuf(f"y{s}", [P, C]) for s in two]
        sg = [st.sbuf(f"sg{s}", [P, FT, C]) for s in two]
        mseps = [st.sbuf(f"mseps{s}", [P, TPC]) for s in two]
        rms = [st.sbuf(f"rms{s}", [P, TPC]) for s in two]
        bank = [[st.psum(f"ps{s}{j}", [P, C]) for j in range(4)] for s in two]
        loaded = st.sem_each("loaded")
        rs = RmsSems(st, "rms")
        attn_ready = st.sem("attn_ready")
        h_ready = st.sem("h_ready")
        gate_ready = st.sem("gate_ready")
        silu_ready = st.sem("silu_ready")
        up_ready = st.sem("up_ready")
        su_ready = st.sem("su_ready")
        down_ready = st.sem("down_ready")
        sum_ready = st.sem("sum_ready")
        done = st.sem("done")

        with nc.Block() as block:

            @block.sync
            def _(sp):
                sp.sem_inc(attn_ready, 1)
                with sp.Fori(0, TRIPS) as trip:
                    t2 = trip * STREAMS
                    for s in two:
                        sp.wait_ge(attn_ready, t2 + 1)
                        sp.dma_start(o[s][:, :], o_dram[:, bass.ds((trip * STREAMS + s) * C, C)]).then_inc(loaded[s], 16)

            @block.gpsimd
            def _(pool):
                with pool.Fori(0, TRIPS) as trip:
                    for s in two:
                        pool.wait_ge(rs.mseps_ready, trip * STREAMS + s + 1)
                        nc.gpsimd.tensor_tensor(rms[s][:, :], mseps[s][:, :], k.minus_half[:, 0:TPC], ALU.pow).then_inc(rs.rms_ready, 1)

            @block.scalar
            def _(act):
                with act.Fori(0, TRIPS) as trip:
                    t2 = trip * STREAMS
                    for s in two:
                        act.wait_ge(h_ready, t2 + s + 1)
                        nc.scalar.activation(sq[s][:, :], h[s][:, :], ACT.Square).then_inc(rs.square_ready, 1)
                    for j in range(FT):
                        for s in two:
                            act.wait_ge(gate_ready, trip * STREAMS * FT + j * STREAMS + s + 1)
                            nc.scalar.activation(sg[s][:, j, :], bank[s][j % 2][:, :], ACT.Silu).then_inc(silu_ready, 1)

            @block.vector
            def _(dve):
                dve.sem_inc(done, 1)
                with dve.Fori(0, TRIPS) as trip:
                    t2 = trip * STREAMS
                    for s in two:
                        dve.wait_ge(attn_ready, t2 + s + 2)
                        nc.vector.tensor_tensor(h[s][:, :], chunk_of(n_all, trip, s), bank[s][0][:, :], ALU.add).then_inc(h_ready, 1)
                    for s in two:
                        dve.wait_ge(rs.ms_ready, t2 + s + 1)
                        nc.vector.tensor_scalar(mseps[s][:, :], bank[s][1][:, 0:TPC], EPS, None, ALU.add).then_inc(rs.mseps_ready, 1)
                    for s in two:
                        dve.wait_ge(rs.spread_ready, t2 + s + 1)
                        nc.vector.scalar_tensor_tensor(y[s][:, :], h[s][:, :], cuts["ln2"], bank[s][0][:, :],
                                                       ALU.mult, ALU.mult).then_inc(rs.normed_ready, 1)
                    for j in range(FT):
                        for s in two:
                            n = trip * STREAMS * FT + j * STREAMS + s + 1
                            dve.wait_ge(silu_ready, n)
                            dve.wait_ge(up_ready, n)
                            nc.vector.tensor_tensor(sg[s][:, j, :], sg[s][:, j, :], bank[s][2][:, :], ALU.mult).then_inc(su_ready, 1)
                    for s in two:
                        dve.wait_ge(down_ready, t2 + s + 1)
                        nc.vector.tensor_tensor(h[s][:, :], h[s][:, :], bank[s][3][:, :], ALU.add).then_inc(sum_ready, 1)
                    for s in two:
                        dve.wait_ge(sum_ready, t2 + s + 1)
                        xs = chunk_of(x, trip, s)
                        nc.vector.tensor_tensor(xs, xs, h[s][:, :], ALU.add).then_inc(done, 1)

            @block.tensor
            def _(pe):
                with pe.Fori(0, TRIPS) as trip:
                    t2 = trip * STREAMS
                    pe.wait_ge(done, t2 + 1)
                    for s in two:
                        pe.wait_ge(loaded[s], trip * 16 + 16)
                        nc.tensor.matmul(bank[s][0][:, :], cuts["wo"], o[s][:, :], start=True, stop=True).then_inc(attn_ready, 1)
                    for s in two:
                        pe.wait_ge(rs.square_ready, t2 + s + 1)
                        for t in range(TPC):
                            mm = nc.tensor.matmul(bank[s][1][:, t:t + 1], sq[s][:, t * P:(t + 1) * P], k.mean[:, 0:1],
                                                  start=True, stop=True)
                        mm.then_inc(rs.ms_ready, 1)
                    for s in two:
                        pe.wait_ge(rs.rms_ready, t2 + s + 1)
                        for t in range(TPC):
                            mm = nc.tensor.transpose(bank[s][0][:, t * P:(t + 1) * P],
                                                     rms[s][:, t:t + 1].to_broadcast([P, P]), k.ident[:, :])
                        mm.then_inc(rs.spread_ready, 1)

                    def down(s):
                        for j in range(FT):
                            pe.wait_ge(su_ready, trip * STREAMS * FT + j * STREAMS + s + 1)
                            mm = nc.tensor.matmul(bank[s][3][:, :], cuts["wd"][:, j * P:(j + 1) * P], sg[s][:, j, :],
                                                  start=j == 0, stop=j == FT - 1)
                        mm.then_inc(down_ready, 1)

                    for j in range(FT):
                        for s in two:
                            n = trip * STREAMS * FT + j * STREAMS + s + 1
                            if j == 0:
                                pe.wait_ge(rs.normed_ready, t2 + s + 1)
                            if j >= 2:
                                pe.wait_ge(silu_ready, n - 2 * STREAMS)
                            nc.tensor.matmul(bank[s][j % 2][:, :], cuts["wg"][:, j * P:(j + 1) * P], y[s][:, :],
                                             start=True, stop=True).then_inc(gate_ready, 1)
                        for s in two:
                            n = trip * STREAMS * FT + j * STREAMS + s + 1
                            if j >= 1:
                                pe.wait_ge(su_ready, n - STREAMS)
                            nc.tensor.matmul(bank[s][2][:, :], cuts["wu"][:, j * P:(j + 1) * P], y[s][:, :],
                                             start=True, stop=True).then_inc(up_ready, 1)
                    for s in two:
                        down(s)


def l2_ffn(nc, k, w_dram, x):
    with Stage(nc, "l2f") as st:
        w = st.sbuf("w", [P, w_dram.shape[1]])
        w_r, w_k, w_v = (w[:, j * P:(j + 1) * P] for j in range(3))
        mu_r, mu_k = w[:, 3 * P:3 * P + 1], w[:, 3 * P + 1:3 * P + 2]
        two = range(STREAMS)
        cen, sq, diff, xr, xk, r, kact = ([st.sbuf(f"{n}{s}", [P, C]) for s in two]
                                          for n in ("cen", "sq", "diff", "xr", "xk", "r", "kact"))
        nz = [st.sbuf(f"nz{s}", [P, SEQ, S + 1]) for s in two]
        vareps, rstd = ([st.sbuf(f"{n}{s}", [P, TPC]) for s in two] for n in ("vareps", "rstd"))
        bank = [[st.psum(f"ps{s}{j}", [P, C]) for j in range(4)] for s in two]
        loaded, zeroed = st.sem("loaded"), st.sem("zeroed")
        ns = NormSems(st)
        diff_ready = st.sem("diff_ready")
        mix_ready = st.sem("mix_ready")
        proj_ready = st.sem("proj_ready")
        relu_ready = st.sem("relu_ready")
        kact_ready = st.sem("kact_ready")
        r_ready = st.sem("r_ready")
        v_ready = st.sem("v_ready")
        out_ready = st.sem("out_ready")
        done = st.sem("done")

        with nc.Block() as block:

            @block.sync
            def _(sp):
                sp.dma_start(w[:, :], w_dram).then_inc(loaded, 16)

            @block.gpsimd
            def _(pool):
                for s in two:
                    nc.gpsimd.memset(nz[s][:, :, 0:1], 0.0).then_inc(zeroed, 1)
                pool.wait_ge(zeroed, STREAMS)
                with pool.Fori(0, TRIPS) as trip:
                    t2 = trip * STREAMS
                    for s in two:
                        norm_pool_rstd(nc, pool, k, ns, t2 + s + 1, vareps[s][:, :], rstd[s][:, :])
                    for s in two:
                        pool.wait_ge(ns.normed_ready, t2 + s + 1)
                        nc.gpsimd.tensor_tensor(seqs(diff[s][:, :]), nz[s][:, :, 1:S + 1], nz[s][:, :, 0:S],
                                                ALU.subtract).then_inc(diff_ready, 1)

            @block.scalar
            def _(act):
                with act.Fori(0, TRIPS) as trip:
                    t2 = trip * STREAMS
                    for s in two:
                        norm_act_square(nc, act, ns, t2 + s + 1, cen[s][:, :], sq[s][:, :])
                    for s in two:
                        act.wait_ge(proj_ready, (t2 + s) * 2 + 1)
                        nc.scalar.activation(kact[s][:, :], bank[s][1][:, :], ACT.Relu).then_inc(relu_ready, 1)
                        act.wait_ge(relu_ready, t2 + s + 1)
                        nc.scalar.activation(kact[s][:, :], kact[s][:, :], ACT.Square).then_inc(kact_ready, 1)
                        act.wait_ge(proj_ready, (t2 + s) * 2 + 2)
                        nc.scalar.activation(r[s][:, :], bank[s][0][:, :], ACT.Sigmoid).then_inc(r_ready, 1)

            @block.vector
            def _(dve):
                dve.sem_inc(done, 1)
                dve.wait_ge(loaded, 16)
                dve.wait_ge(zeroed, STREAMS)
                with dve.Fori(0, TRIPS) as trip:
                    t2 = trip * STREAMS
                    for s in two:
                        norm_dve_centre(nc, dve, ns, t2 + s + 1, chunk_of(x, trip, s), bank[s][0][:, :], cen[s][:, :])
                    for s in two:
                        norm_dve_vareps(nc, dve, ns, t2 + s + 1, bank[s][1][:, :], vareps[s][:, :], 1e-5)
                    for s in two:
                        norm_dve_scale(nc, dve, ns, t2 + s + 1, seqs(cen[s][:, :]), 1.0, seqs(bank[s][0][:, :]),
                                       nz[s][:, :, 1:S + 1])
                    for s in two:
                        dve.wait_ge(diff_ready, t2 + s + 1)
                        for dst, mu in ((xk, mu_k), (xr, mu_r)):
                            nc.vector.scalar_tensor_tensor(seqs(dst[s][:, :]), seqs(diff[s][:, :]), mu, nz[s][:, :, 0:S],
                                                           ALU.mult, ALU.add).then_inc(mix_ready, 1)
                    for s in two:
                        dve.wait_ge(v_ready, t2 + s + 1)
                        dve.wait_ge(r_ready, t2 + s + 1)
                        nc.vector.tensor_tensor(r[s][:, :], r[s][:, :], bank[s][2][:, :], ALU.mult).then_inc(out_ready, 1)
                    for s in two:
                        dve.wait_ge(out_ready, t2 + s + 1)
                        xs = chunk_of(x, trip, s)
                        nc.vector.tensor_tensor(xs, xs, r[s][:, :], ALU.add).then_inc(done, 1)

            @block.tensor
            def _(pe):
                pe.wait_ge(loaded, 16)
                with pe.Fori(0, TRIPS) as trip:
                    t2 = trip * STREAMS
                    pe.wait_ge(done, t2 + 1)
                    for s in two:
                        norm_pe_mean(nc, k, ns, chunk_of(x, trip, s), bank[s][0][:, :])
                    for s in two:
                        norm_pe_var(nc, pe, k, ns, t2 + s + 1, sq[s][:, :], bank[s][1][:, :])
                    for s in two:
                        norm_pe_spread(nc, pe, k, ns, t2 + s + 1, rstd[s][:, :], bank[s][0][:, :])
                    for s in two:
                        for i, (wt, src, b) in enumerate(((w_k, xk, 1), (w_r, xr, 0))):
                            pe.wait_ge(mix_ready, (t2 + s) * 2 + i + 1)
                            nc.tensor.matmul(bank[s][b][:, :], wt, src[s][:, :], start=True, stop=True).then_inc(proj_ready, 1)
                    for s in two:
                        pe.wait_ge(kact_ready, t2 + s + 1)
                        nc.tensor.matmul(bank[s][2][:, :], w_v, kact[s][:, :], start=True, stop=True).then_inc(v_ready, 1)


def l3_attention(nc, k, w_dram, x):
    NH, DK, L, R = 8, 128, 32, 32
    QA, KA = L + 1, L + R + 1
    SCALE = 1.0 / float(DK + R) ** 0.5
    HP = NH // 2
    UNITS = SEQ * 2 * HP
    RING = 4
    HG = NH // 4
    with Stage(nc, "l3a") as st:
        w = st.sbuf("w", [P, w_dram.shape[1]])
        cuts, o = {}, 0
        for name, width in (("uq", NH * QA), ("uk", NH * QA), ("qr", NH * R), ("dq", L), ("dkv_kr", L + R),
                            ("uv", NH * P), ("o", NH * P), ("b_dq", 1), ("b_k", 1), ("b_uv", NH), ("b_o", 1),
                            ("b_dkv", L)):
            cuts[name] = w[:, o:o + width]
            o += width
        gmat = st.sbuf("gmat", [QA, NH, KA])
        vo = st.sbuf("vo", [P, HG, P])
        bias = st.sbuf("bias", [P, 1])
        cen, sq, n_ = (st.sbuf(n, [P, C]) for n in ("cen", "sq", "n"))
        vareps, rstd = (st.sbuf(n, [P, TPC]) for n in ("vareps", "rstd"))
        cq = st.sbuf("cq", [QA, C])
        key = st.sbuf("key", [KA, C])
        lat = st.sbuf("lat", [P, TPC, QA])
        qe = st.sbuf("qe", [KA, NH, C])
        mx = st.sbuf("mx", [P, TPC, NH])
        negmax = st.sbuf("negmax", [P, TPC, NH, KA])
        probs = st.sbuf("probs", [P, UNITS, C])
        rsum = st.sbuf("rsum", [P, TPC, NH])
        ctxn = st.sbuf("ctxn", [P, TPC, NH, L])
        ctxT = st.sbuf("ctxT", [P, HG, C])
        bank = [st.psum(f"ps{j}", [P, C]) for j in range(8)]

        loaded, const_ready = st.sem("loaded"), st.sem("const_ready")
        folded_ps, folded = st.sem("folded_ps"), st.sem("folded")
        ns = NormSems(st)
        lat_ready = st.sem("lat_ready")
        cq_ready = st.sem("cq_ready")
        key_ready = st.sem("key_ready")
        lat_copied = st.sem("lat_copied")
        q_ready = st.sem("q_ready")
        q_act, q_dve = st.sem("q_act"), st.sem("q_dve")
        score_ready = st.sem("score_ready")
        max_done = st.sem("max_done")
        negmax_ready = st.sem("negmax_ready")
        negT_ready = st.sem("negT_ready")
        qmax_ready = st.sem("qmax_ready")
        scoreT_ready = st.sem("scoreT_ready")
        exp_done = st.sem("exp_done")
        ctx_ready = st.sem("ctx_ready")
        rsum_ready = st.sem("rsum_ready")
        ctxn_ready = st.sem("ctxn_ready")
        ctxT_ready = st.sem("ctxT_ready")
        ctxT_copied = st.sem("ctxT_copied")
        out_ready = st.sem("out_ready")
        done = st.sem("done")

        with nc.Block() as block:

            @block.sync
            def _(sp):
                sp.dma_start(w[:, :], w_dram).then_inc(loaded, 16)

            @block.gpsimd
            def _(pool):
                nc.gpsimd.memset(cq[:, :], 1.0).then_inc(const_ready, 1)
                nc.gpsimd.memset(key[:, :], 1.0).then_inc(const_ready, 1)
                nc.gpsimd.memset(lat[:, :, :], 1.0).then_inc(const_ready, 1)
                nc.gpsimd.memset(negmax[:, :, :, :], 0.0).then_inc(const_ready, 1)
                with pool.Fori(0, NCH) as trip:
                    norm_pool_rstd(nc, pool, k, ns, trip + 1, vareps[:, :], rstd[:, :])

            @block.scalar
            def _(act):
                act.wait_ge(loaded, 16)
                with act.Fori(0, NCH) as trip:
                    norm_act_square(nc, act, ns, trip + 1, cen[:, :], sq[:, :])
                    act.wait_ge(lat_ready, trip * 3 + 1)
                    nc.scalar.activation(cq[0:L, :], bank[0][0:L, :], ACT.Identity, bias=cuts["b_dq"][0:L, :]).then_inc(cq_ready, 1)
                    act.wait_ge(lat_ready, trip * 3 + 2)
                    nc.scalar.activation(key[0:L + R, :], bank[1][0:L + R, :], ACT.Identity,
                                         bias=cuts["b_k"][0:L + R, :]).then_inc(key_ready, 1)
                    for h in range(0, NH, 2):
                        act.wait_ge(q_ready, trip * NH + h + 1)
                        nc.scalar.activation(qe[:, h, :], bank[3 + h % 4][0:KA, :], ACT.Copy).then_inc(q_act, 1)
                    for u in range(UNITS):
                        act.wait_ge(scoreT_ready, trip * UNITS + u + 1)
                        nc.scalar.activation(probs[:, u, :], bank[u % RING][:, :], ACT.Exp).then_inc(exp_done, 1)
                    for g in range(HG):
                        act.wait_ge(ctxT_ready, trip * HG + g + 1)
                        nc.scalar.activation(ctxT[:, g, :], bank[g][:, :], ACT.Copy).then_inc(ctxT_copied, 1)

            @block.vector
            def _(dve):
                dve.sem_inc(done, 1)
                dve.wait_ge(loaded, 16)
                dve.wait_ge(const_ready, 4)
                for h in range(NH):
                    dve.wait_ge(folded_ps, h + 1)
                    ps = bank[h % 4]
                    nc.vector.tensor_scalar(gmat[:, h, 0:L], ps[0:QA, 0:L], SCALE, None, ALU.mult)
                    nc.vector.tensor_scalar(gmat[:, h, L + R:KA], ps[0:QA, L:QA], SCALE, None, ALU.mult)
                    nc.vector.tensor_scalar(gmat[:, h, L:L + R], cuts["qr"][0:QA, h * R:(h + 1) * R], SCALE, None,
                                            ALU.mult).then_inc(folded, 1)
                for g in range(HG):
                    dve.wait_ge(folded_ps, NH + g + 1)
                    nc.vector.tensor_copy(vo[:, g, :], bank[4 + g][:, 0:P])
                dve.wait_ge(folded_ps, NH + HG + 1)
                nc.vector.tensor_tensor(bias[:, :], bank[6][:, 0:1], cuts["b_o"], ALU.add).then_inc(folded, 1)
                dve.wait_ge(folded, NH + 1)
                with dve.Fori(0, NCH) as trip:
                    norm_dve_centre(nc, dve, ns, trip + 1, chunk_at(x, trip), bank[6][:, :], cen[:, :])
                    norm_dve_vareps(nc, dve, ns, trip + 1, bank[7][:, :], vareps[:, :], 1e-5)
                    norm_dve_scale(nc, dve, ns, trip + 1, cen[:, :], 1.0, bank[6][:, :], n_[:, :])
                    dve.wait_ge(lat_ready, trip * 3 + 3)
                    nc.vector.tensor_tensor(lat[:, :, 0:L], bank[2][:, 0:TPC * L].rearrange("p (t c) -> p t c", c=L),
                                            bcast(cuts["b_dkv"], 1, TPC), ALU.add).then_inc(lat_copied, 1)
                    for h in range(1, NH, 2):
                        dve.wait_ge(q_ready, trip * NH + h + 1)
                        nc.vector.tensor_copy(qe[:, h, :], bank[3 + h % 4][0:KA, :]).then_inc(q_dve, 1)
                    for u in range(UNITS):
                        t, hp = u // HP, u % HP
                        dve.wait_ge(score_ready, trip * UNITS + u + 1)
                        nc.vector.tensor_reduce(mx[:, t, 2 * hp:2 * hp + 2],
                                                bank[u % RING][:, :].rearrange("p (h c) -> p h c", h=2),
                                                AX.X, ALU.max).then_inc(max_done, 1)
                    dve.wait_ge(max_done, (trip + 1) * UNITS)
                    nc.vector.tensor_scalar(negmax[:, :, :, KA - 1], mx[:, :, :], -1.0, None, ALU.mult).then_inc(negmax_ready, 1)
                    for i in range(2 * TPC):
                        t, h0 = i // 2, i % 2 * 4
                        dve.wait_ge(negT_ready, trip * 2 * TPC + i + 1)
                        row = qe[KA - 1:KA, h0:h0 + 4, t * P:(t + 1) * P]
                        nc.vector.tensor_tensor(row, row, bank[4 + i % 4][KA - 1:KA, :].rearrange("p (h c) -> p h c", h=4),
                                                ALU.add).then_inc(qmax_ready, 1)
                    for t in range(TPC):
                        cx = bank[4 + t % 2][:, 0:NH * QA].rearrange("p (h c) -> p h c", h=NH)
                        dve.wait_ge(ctx_ready, trip * TPC + t + 1)
                        nc.vector.reciprocal(rsum[:, t, :], cx[:, :, L]).then_inc(rsum_ready, 1)
                        dve.wait_ge(rsum_ready, trip * TPC + t + 1)
                        nc.vector.tensor_tensor(ctxn[:, t, :, :], cx[:, :, 0:L], bcast(rsum[:, t, :], 2, L),
                                                ALU.mult).then_inc(ctxn_ready, 1)
                    dve.wait_ge(out_ready, trip + 1)
                    xs = chunk_at(x, trip)
                    nc.vector.scalar_tensor_tensor(xs, bank[6][:, :], bias[:, :], xs, ALU.add, ALU.add).then_inc(done, 1)

            @block.tensor
            def _(pe):
                pe.wait_ge(loaded, 16)
                for h in range(NH):
                    if h >= 4:
                        pe.wait_ge(folded, h - 3)
                    nc.tensor.matmul(bank[h % 4][0:QA, 0:QA], cuts["uq"][:, h * QA:(h + 1) * QA],
                                     cuts["uk"][:, h * QA:(h + 1) * QA], start=True, stop=True).then_inc(folded_ps, 1)
                for g in range(HG):
                    for j in range(4):
                        h = g * 4 + j
                        mm = nc.tensor.matmul(bank[4 + g][:, 0:P], cuts["uv"][:, h * P:(h + 1) * P],
                                              cuts["o"][:, h * P:(h + 1) * P], start=j == 0, stop=j == 3)
                    mm.then_inc(folded_ps, 1)
                for h in range(NH):
                    mm = nc.tensor.matmul(bank[6][:, 0:1], cuts["o"][:, h * P:(h + 1) * P], cuts["b_uv"][:, h:h + 1],
                                          start=h == 0, stop=h == NH - 1)
                mm.then_inc(folded_ps, 1)
                pe.wait_ge(folded, NH + 1)
                with pe.Fori(0, NCH) as trip:
                    units = trip * UNITS
                    pe.wait_ge(done, trip + 1)
                    norm_pe_mean(nc, k, ns, chunk_at(x, trip), bank[6][:, :])
                    norm_pe_var(nc, pe, k, ns, trip + 1, sq[:, :], bank[7][:, :])
                    norm_pe_spread(nc, pe, k, ns, trip + 1, rstd[:, :], bank[6][:, :])
                    pe.wait_ge(ns.normed_ready, trip + 1)
                    nc.tensor.matmul(bank[0][0:L, :], cuts["dq"], n_[:, :], start=True, stop=True).then_inc(lat_ready, 1)
                    nc.tensor.matmul(bank[1][0:L + R, :], cuts["dkv_kr"], n_[:, :], start=True, stop=True).then_inc(lat_ready, 1)
                    for t in range(TPC):
                        mm = nc.tensor.matmul(bank[2][:, t * L:(t + 1) * L], n_[:, t * P:(t + 1) * P],
                                              cuts["dkv_kr"][:, 0:L], start=True, stop=True)
                    mm.then_inc(lat_ready, 1)
                    pe.wait_ge(cq_ready, trip + 1)
                    for h in range(NH):
                        if h >= 4:
                            pe.wait_ge((q_act, q_dve)[h % 2], trip * (NH // 2) + (h - 4) // 2 + 1)
                        nc.tensor.matmul(bank[3 + h % 4][0:KA, :], gmat[:, h, :], cq[:, :], start=True, stop=True).then_inc(q_ready, 1)
                    pe.wait_ge(key_ready, trip + 1)
                    pe.wait_ge(lat_copied, trip + 1)
                    pe.wait_ge(q_act, (trip + 1) * (NH // 2))
                    pe.wait_ge(q_dve, (trip + 1) * (NH // 2))
                    for u in range(UNITS):
                        t, hp = u // HP, u % HP
                        b = t // 2
                        if u >= RING:
                            pe.wait_ge(max_done, units + u - RING + 1)
                        for i in range(2):
                            mm = nc.tensor.matmul(bank[u % RING][:, i * S:(i + 1) * S], qe[:, 2 * hp + i, t * P:(t + 1) * P],
                                                  key[:, b * S:(b + 1) * S], start=True, stop=True)
                        mm.then_inc(score_ready, 1)
                    pe.wait_ge(negmax_ready, trip + 1)
                    for i in range(2 * TPC):
                        t, h0 = i // 2, i % 2 * 4
                        if i >= 4:
                            pe.wait_ge(qmax_ready, trip * 2 * TPC + i - 3)
                        for j in range(4):
                            mm = nc.tensor.matmul(bank[4 + i % 4][0:KA, j * P:(j + 1) * P], negmax[:, t, h0 + j, :],
                                                  k.ident[:, :], start=True, stop=True)
                        mm.then_inc(negT_ready, 1)
                    pe.wait_ge(qmax_ready, (trip + 1) * 2 * TPC)
                    for u in range(UNITS):
                        t, hp = u // HP, u % HP
                        b = t // 2
                        if u >= RING:
                            pe.wait_ge(exp_done, units + u - RING + 1)
                        nc.tensor.matmul(bank[u % RING][:, :], key[:, t * P:(t + 1) * P],
                                         qe[:, 2 * hp:2 * hp + 2, b * S:(b + 1) * S],
                                         start=True, stop=True).then_inc(scoreT_ready, 1)
                    for t in range(TPC):
                        b, qt = t // 2, t % 2
                        pe.wait_ge(exp_done, units + (b + 1) * 2 * HP)
                        if t >= 2:
                            pe.wait_ge(ctxn_ready, trip * TPC + t - 1)
                        for h in range(NH):
                            for kt in range(2):
                                pr = probs[:, (2 * b + kt) * HP + h // 2, :]
                                c0 = h % 2 * S + qt * P
                                mm = nc.tensor.matmul(bank[4 + t % 2][:, h * QA:(h + 1) * QA], pr[:, c0:c0 + P],
                                                      lat[:, 2 * b + kt, :], start=kt == 0, stop=kt == 1)
                        mm.then_inc(ctx_ready, 1)
                    pe.wait_ge(exp_done, units + UNITS)
                    pe.wait_ge(ctxn_ready, (trip + 1) * TPC)
                    for g in range(HG):
                        for t in range(TPC):
                            mm = nc.tensor.transpose(bank[g][:, t * P:(t + 1) * P],
                                                     ctxn[:, t, g * 4:(g + 1) * 4, :].rearrange("p h c -> p (h c)"),
                                                     k.ident[:, :])
                        mm.then_inc(ctxT_ready, 1)
                    for g in range(HG):
                        pe.wait_ge(ctxT_copied, trip * HG + g + 1)
                        mm = nc.tensor.matmul(bank[6][:, :], vo[:, g, :], ctxT[:, g, :], start=g == 0, stop=g == HG - 1)
                    mm.then_inc(out_ready, 1)


def l3_ffn(nc, k, w_dram, x):
    E, INTER, GROUPS, TOPG, TOPK = 16, 64, 4, 2, 4
    PER = E // GROUPS
    PAIRS = E // 2
    STEPS = PAIRS + 1
    with Stage(nc, "l3f") as st:
        w = st.sbuf("w", [P, w_dram.shape[1]])
        cuts, o = {}, 0
        for name, width in (("gate", E), ("w1", E * INTER), ("w3", E * INTER), ("w2", PAIRS * P),
                            ("s1", INTER), ("s3", INTER), ("s2", P), ("gbias", E)):
            cuts[name] = w[:, o:o + width]
            o += width
        two = range(STREAMS)
        expand = st.sbuf("expand", [E, PAIRS, 2, INTER])
        cen, sq, n_ = ([st.sbuf(f"{n}{s}", [P, C]) for s in two] for n in ("cen", "sq", "n"))
        vareps, rstd = ([st.sbuf(f"{n}{s}", [P, TPC]) for s in two] for n in ("vareps", "rstd"))
        th, so, sb_, comb, rank = ([st.sbuf(f"{n}{s}", [P, TPC, E]) for s in two]
                                   for n in ("th", "so", "sb", "comb", "rank"))
        gm, grank = ([st.sbuf(f"{n}{s}", [P, TPC, GROUPS]) for s in two] for n in ("gm", "grank"))
        gt, eq = ([st.sbuf(f"{n}{s}", [P, TPC, E, E]) for s in two] for n in ("gt", "eq"))
        combT = [st.sbuf(f"combT{s}", [E, C]) for s in two]
        hid = [st.sbuf(f"hid{s}", [P, 2, C]) for s in two]
        bank = [[st.psum(f"ps{s}{j}", [P, C]) for j in range(4)] for s in two]
        loaded, const_step = st.sem("loaded"), st.sem("const_step")
        ns = NormSems(st)
        logits_ready = st.sem("logits_ready")
        tanh_ready = st.sem("tanh_ready")
        comb_ready = st.sem("comb_ready")
        combT_ready = st.sem("combT_ready")
        combT_copied = st.sem("combT_copied")
        inner_ready = st.sem_each("inner")
        silu_ready = st.sem_each("silu")
        prod_ready = st.sem_each("prod")
        hid_ready = st.sem_each("hid")
        down_ready = st.sem_each("down")
        done = st.sem("done")
        dve_step = st.sem("dve_step")

        with nc.Block() as block:

            @block.sync
            def _(sp):
                sp.dma_start(w[:, :], w_dram).then_inc(loaded, 16)

            @block.gpsimd
            def _(pool):
                nc.gpsimd.memset(expand[:, :, :, :], 0.0).then_inc(const_step, 1)
                pool.wait_ge(const_step, 1)
                nc.gpsimd.affine_select(out=expand[:, :, :, :], in_=expand[:, :, :, :], compare_op=ALU.not_equal,
                                        fill=1.0, base=0, pattern=[[-2, PAIRS], [-1, 2], [0, INTER]],
                                        channel_multiplier=1).then_inc(const_step, 1)
                with pool.Fori(0, TRIPS) as trip:
                    for s in two:
                        norm_pool_rstd(nc, pool, k, ns, trip * STREAMS + s + 1, vareps[s][:, :], rstd[s][:, :])

            @block.scalar
            def _(act):
                with act.Fori(0, TRIPS) as trip:
                    t2 = trip * STREAMS
                    for s in two:
                        norm_act_square(nc, act, ns, t2 + s + 1, cen[s][:, :], sq[s][:, :])
                    for s in two:
                        act.wait_ge(logits_ready, t2 + s + 1)
                        nc.scalar.activation(th[s][:, :, :], bank[s][1][:, 0:TPC * E].rearrange("p (t e) -> p t e", e=E),
                                             ACT.Tanh, scale=0.5).then_inc(tanh_ready, 1)
                    for s in two:
                        act.wait_ge(combT_ready, t2 + s + 1)
                        nc.scalar.activation(combT[s][:, :], bank[s][2][0:E, :], ACT.Copy).then_inc(combT_copied, 1)
                    for p in range(STEPS):
                        for s in two:
                            n = trip * STEPS + p
                            rows = P if p < PAIRS else INTER
                            act.wait_ge(inner_ready[s], n * 3 + 1)
                            if p >= 2:
                                act.wait_ge(down_ready[s], n - 1)
                            nc.scalar.activation(hid[s][0:rows, p % 2, :], bank[s][0][0:rows, :], ACT.Silu).then_inc(silu_ready[s], 1)

            @block.vector
            def _(dve):
                dve.sem_inc(done, 1)
                dve.wait_ge(loaded, 16)
                with dve.Fori(0, TRIPS) as trip:
                    t2 = trip * STREAMS
                    ch = Chain(dve, dve_step, trip, STREAMS * (5 + 2 * RANK_MARKS))
                    for s in two:
                        norm_dve_centre(nc, dve, ns, t2 + s + 1, chunk_of(x, trip, s), bank[s][0][:, :], cen[s][:, :])
                    for s in two:
                        norm_dve_vareps(nc, dve, ns, t2 + s + 1, bank[s][1][:, :], vareps[s][:, :], 1e-5)
                    for s in two:
                        norm_dve_scale(nc, dve, ns, t2 + s + 1, cen[s][:, :], 1.0, bank[s][0][:, :], n_[s][:, :])
                    for s in two:
                        def step(op):
                            ch.wait(ch.mark(op))

                        dve.wait_ge(tanh_ready, t2 + s + 1)
                        step(nc.vector.tensor_scalar(so[s][:, :, :], th[s][:, :, :], 0.5, 0.5, ALU.mult, ALU.add))
                        step(nc.vector.tensor_tensor(sb_[s][:, :, :], so[s][:, :, :], bcast(cuts["gbias"], 1, TPC), ALU.add))
                        grouped = sb_[s][:, :, :].rearrange("p t (g e) -> p t g e", g=GROUPS)
                        step(nc.vector.tensor_reduce(gm[s][:, :, :], grouped, AX.X, ALU.max))
                        r = rank_by_value(nc, ch, k, gm[s][:, :, :], gt[s][:, :, 0:GROUPS, 0:GROUPS],
                                          eq[s][:, :, 0:GROUPS, 0:GROUPS], grank[s][:, :, :], TPC, GROUPS)
                        ch.wait(r)
                        step(nc.vector.tensor_scalar(grank[s][:, :, :], grank[s][:, :, :], float(TOPG), -1e30, ALU.is_ge, ALU.mult))
                        step(nc.vector.tensor_tensor(grouped, grouped, bcast(grank[s][:, :, :], 3, PER), ALU.add))
                        r = rank_by_value(nc, ch, k, sb_[s][:, :, :], gt[s][:, :, :, :], eq[s][:, :, :, :],
                                          rank[s][:, :, :], TPC, E)
                        ch.wait(r)
                        nc.vector.scalar_tensor_tensor(comb[s][:, :, :], rank[s][:, :, :], float(TOPK), so[s][:, :, :],
                                                       ALU.is_lt, ALU.mult).then_inc(comb_ready, 1)
                    for p in range(STEPS):
                        for s in two:
                            n = trip * STEPS + p
                            rows = P if p < PAIRS else INTER
                            hp = hid[s][0:rows, p % 2, :]
                            dve.wait_ge(inner_ready[s], n * 3 + 3)
                            dve.wait_ge(silu_ready[s], n + 1)
                            if p < PAIRS:
                                nc.vector.tensor_tensor(hp, hp, bank[s][1][0:rows, :], ALU.mult).then_inc(prod_ready[s], 1)
                                dve.wait_ge(prod_ready[s], trip * PAIRS + p + 1)
                                nc.vector.tensor_tensor(hp, hp, bank[s][2][0:rows, :], ALU.mult).then_inc(hid_ready[s], 1)
                            else:
                                nc.vector.tensor_tensor(hp, hp, bank[s][1][0:rows, :], ALU.mult).then_inc(hid_ready[s], 1)
                    for s in two:
                        dve.wait_ge(down_ready[s], (trip + 1) * STEPS)
                        xs = chunk_of(x, trip, s)
                        nc.vector.tensor_tensor(xs, xs, bank[s][3][:, :], ALU.add).then_inc(done, 1)
                    ch.close()

            @block.tensor
            def _(pe):
                pe.wait_ge(loaded, 16)
                pe.wait_ge(const_step, 2)
                with pe.Fori(0, TRIPS) as trip:
                    t2 = trip * STREAMS
                    pe.wait_ge(done, t2 + 1)
                    for s in two:
                        norm_pe_mean(nc, k, ns, chunk_of(x, trip, s), bank[s][0][:, :])
                    for s in two:
                        norm_pe_var(nc, pe, k, ns, t2 + s + 1, sq[s][:, :], bank[s][1][:, :])
                    for s in two:
                        norm_pe_spread(nc, pe, k, ns, t2 + s + 1, rstd[s][:, :], bank[s][0][:, :])
                    for s in two:
                        pe.wait_ge(ns.normed_ready, t2 + s + 1)
                        for t in range(TPC):
                            mm = nc.tensor.matmul(bank[s][1][:, t * E:(t + 1) * E], n_[s][:, t * P:(t + 1) * P],
                                                  cuts["gate"], start=True, stop=True)
                        mm.then_inc(logits_ready, 1)
                    for s in two:
                        pe.wait_ge(comb_ready, t2 + s + 1)
                        for t in range(TPC):
                            mm = nc.tensor.matmul(bank[s][2][0:E, t * P:(t + 1) * P], comb[s][:, t, :], k.ident[:, :],
                                                  start=True, stop=True)
                        mm.then_inc(combT_ready, 1)

                    def inner(p, s):
                        n = trip * STEPS + p
                        shared = p == PAIRS
                        rows, c0 = (INTER, 0) if shared else (P, p * P)
                        a, b = ("s1", "s3") if shared else ("w1", "w3")
                        if p == 0:
                            pe.wait_ge(combT_copied, t2 + s + 1)
                        else:
                            pe.wait_ge(silu_ready[s], n)
                        nc.tensor.matmul(bank[s][0][0:rows, :], cuts[a][:, c0:c0 + rows], n_[s][:, :],
                                         start=True, stop=True).then_inc(inner_ready[s], 1)
                        if p:
                            pe.wait_ge(hid_ready[s], n)
                        nc.tensor.matmul(bank[s][1][0:rows, :], cuts[b][:, c0:c0 + rows], n_[s][:, :],
                                         start=True, stop=True).then_inc(inner_ready[s], 2 if shared else 1)
                        if not shared:
                            nc.tensor.matmul(bank[s][2][:, :], expand[:, p, :, :].rearrange("e a i -> e (a i)"),
                                             combT[s][:, :], start=True, stop=True).then_inc(inner_ready[s], 1)

                    def down(p, s):
                        pe.wait_ge(hid_ready[s], trip * STEPS + p + 1)
                        rows, wt = (P, cuts["w2"][:, p * P:(p + 1) * P]) if p < PAIRS else (INTER, cuts["s2"])
                        nc.tensor.matmul(bank[s][3][:, :], wt[0:rows, :], hid[s][0:rows, p % 2, :],
                                         start=p == 0, stop=p == PAIRS).then_inc(down_ready[s], 1)

                    for p in range(STEPS):
                        inner(p, 0)
                        if p:
                            down(p - 1, 1)
                        inner(p, 1)
                        down(p, 0)
                    down(PAIRS, 1)


class Persistent:
    pass


def build(nc, args, out, stages):
    with ExitStack() as ctx:
        k = Persistent()
        x = ctx.enter_context(nc.sbuf_tensor("x", [P, TOK], FP32))
        k.mean = ctx.enter_context(nc.sbuf_tensor("mean_matrix", [P, P], FP32))
        k.ident = ctx.enter_context(nc.sbuf_tensor("identity", [P, P], FP32))
        k.minus_half = ctx.enter_context(nc.sbuf_tensor("minus_half", [P, P], FP32))
        k.lower = ctx.enter_context(nc.sbuf_tensor("lower", [P, 16, 16], FP32))
        with Stage(nc, "load") as st:
            x_loaded = st.sem("x_loaded")
            with nc.Block() as block:

                @block.sync
                def _(sp):
                    sp.dma_start(x[:, :], args["x"]).then_inc(x_loaded, 16)
                    sp.wait_ge(x_loaded, 16)
        make_constants(nc, k)
        for name in stages:
            STAGES[name](nc, k, args[name], x)
        with Stage(nc, "store") as st:
            x_stored = st.sem("x_stored")
            with nc.Block() as block:

                @block.sync
                def _(sp):
                    sp.dma_start(out, x[:, :]).then_inc(x_stored, 16)
                    sp.wait_ge(x_stored, 16)


STAGES = {"l0_attention": l0_attention, "l0_ffn": l0_ffn, "l1_attention": l1_attention, "l1_ffn": l1_ffn,
          "l2_attention": l2_attention, "l2_ffn": l2_ffn, "l3_attention": l3_attention, "l3_ffn": l3_ffn}
ORDER = list(STAGES)


def layouts(i):
    import numpy as np
    cat = lambda parts: np.ascontiguousarray(np.concatenate(parts, axis=1))
    lhs = lambda a: np.transpose(a, (1, 0, 2)).reshape(a.shape[1], -1)
    col = lambda a: np.ascontiguousarray(a.reshape(-1, P).T)
    i = {n: np.asarray(a) for n, a in i.items()}
    d = {"x": np.ascontiguousarray(i["L0_attn_x"].reshape(TOK, P).T)}
    a = lambda n: i["L0_attn_" + n]
    d["l0_attention"] = cat([lhs(a("Wq")), lhs(a("Wk")), lhs(a("Wv")), lhs(a("Wo")), lhs(a("W1")),
                             lhs(a("W2").reshape(16, P, P))]
                            + [col(a(n)) for n in ("bq", "bk", "bv", "bo", "ln1_s", "ln1_b", "b1", "b2", "ln2_s", "ln2_b")])
    rows = lambda a: np.concatenate([a, np.zeros((P - a.shape[0],) + a.shape[1:], a.dtype)])
    every = lambda a: np.broadcast_to(a.reshape(1, -1), (P, a.size))
    a = lambda n: i["L0_ffn_" + n]
    d["l0_ffn"] = cat([a("weight").T, a("lora_A").reshape(-1, P).T, a("gate_w").T,
                       rows(a("lora_B").transpose(0, 2, 1).reshape(-1, P)), col(a("bias")), every(a("gate_b"))])
    a = lambda n: i["L1_attn_" + n]
    heads = 16
    tiled = lambda m: rows(np.tile(m, (1, heads)))
    d["l1_attention"] = cat([tiled(a("W_DQ")), tiled(a("W_UQ").T), tiled(a("W_DKV")), tiled(a("W_UKV")[:8].T),
                             tiled(a("W_KR")), tiled(a("W_QR")), rows(a("W_UKV")[8:]), tiled(a("W_O").T),
                             np.tile(a("q_norm_w"), heads)[:, None], np.tile(a("k_norm_w"), heads)[:, None]])
    a = lambda n: i["L1_ffn_" + n]
    w1 = np.concatenate([a("W1"), a("Ws1")[None]])
    w2 = np.concatenate([a("W2"), a("Ws2")[None]])
    d["l1_ffn"] = cat([a("gate_weight").T, lhs(w1), lhs(w2.reshape(-1, P, P)),
                       col(np.concatenate([a("b1"), a("bs1")[None]])), col(np.concatenate([a("b2"), a("bs2")[None]]))])
    a = lambda n: i["L2_attn_" + n]
    by_dim = lambda m: m.reshape(m.shape[0], 16, 8).transpose(0, 2, 1).reshape(m.shape[0], -1)
    d["l2_attention"] = cat([by_dim(a("Wq")), by_dim(a("Wk")), by_dim(a("Wv")), a("Wb"), by_dim(a("Wo").T).T,
                             a("Wg"), a("Wu"), lhs(a("Wd").reshape(4, P, P)), a("ln1")[:, None], a("ln2")[:, None]])
    a = lambda n: i["L2_ffn_" + n]
    d["l2_ffn"] = cat([a("W_r").T, a("W_k").T, a("W_v").T, a("mu_r")[:, None], a("mu_k")[:, None]])
    a = lambda n: i["L3_attn_" + n]
    aug = lambda m, b: np.concatenate([m, b[None]])
    by_head = lambda m: m.reshape(m.shape[0], 8, P).transpose(2, 1, 0)
    uv = np.zeros((P, 8, 4, 32), np.float32)
    for h in range(8):
        uv[:, h, h % 4] = by_head(a("W_UV"))[:, h]
    d["l3_attention"] = cat([by_head(aug(a("W_UQ"), a("b_UQ"))).reshape(P, -1),
                             by_head(aug(a("W_UK"), a("b_UK"))).reshape(P, -1),
                             rows(aug(a("W_QR"), a("b_QR"))), a("W_DQ"), a("W_DKV"), a("W_KR"), uv.reshape(P, -1),
                             lhs(a("W_O").reshape(8, P, P)), rows(a("b_DQ")[:, None]),
                             rows(np.concatenate([a("b_DKV"), a("b_KR")])[:, None]), col(a("b_UV")),
                             a("b_O")[:, None], every(a("b_DKV"))])
    a = lambda n: i["L3_ffn_" + n]
    d["l3_ffn"] = cat([a("gate_w").T, a("w1").reshape(-1, P).T, a("w3").reshape(-1, P).T,
                       lhs(a("w2").transpose(0, 2, 1).reshape(8, P, P)), a("ws1").T, a("ws3").T, rows(a("ws2").T),
                       every(a("gate_bias"))])
    return d


def kernel(**inputs):
    import numpy as np
    import concourse.bacc as bacc
    from concourse.bass_utils import run_bass_kernel_spmd

    nc = bacc.Bacc("TRN2", target_bir_lowering=False, num_devices=1)
    arrays = layouts(inputs)
    args = {n: nc.dram_tensor(f"in_{n}", a.shape, FP32, kind="ExternalInput").ap() for n, a in arrays.items()}
    out = nc.dram_tensor("out_xt", (P, TOK), FP32, kind="ExternalOutput").ap()
    build(nc, args, out, ORDER)
    r = run_bass_kernel_spmd(nc, [{f"in_{n}": a for n, a in arrays.items()}], core_ids=[0])
    return np.ascontiguousarray(np.asarray(r.results[0]["out_xt"]).T).reshape(B, S, P)
```
